# Optimizing a Trainium2 kernel written in Bass

```python
import numpy as np
import jax
import jax.numpy as jnp

def _softmax(x, axis=-1):
    return jax.nn.softmax(x, axis=axis)

def _gelu(x):
    return jax.nn.gelu(x, approximate=True)

def _silu(x):
    return jax.nn.silu(x)

def _sigmoid(x):
    return jax.nn.sigmoid(x)

def _layernorm(x, axis=-1, eps=1e-05):
    m = jnp.mean(x, axis=axis, keepdims=True)
    v = jnp.var(x, axis=axis, keepdims=True)
    return (x - m) / jnp.sqrt(v + eps)

def _scatter_add(tgt, idx, src, axis=0):
    return tgt.at[idx].add(src)

def _segment_sum(src, seg, n):
    return jax.ops.segment_sum(src, seg, n)
kernel_name = 'mk_adaln_ffn_d1_seqx_r8_fa4d2c'

def setup_inputs(seed: int=0):
    np.random.seed(seed)
    _w = jnp.asarray

    def _rec_inputs():
        import jax
        import jax.numpy as jnp
        _rk = jax.random.key(seed)
        x = -0.000125 + 0.9999 * jax.random.normal(jax.random.fold_in(_rk, 1), (128, 32, 512), jnp.float32)
        _lenS = 32 - jax.random.randint(jax.random.fold_in(_rk, 7), (128,), 0, max(1, 32 // 4) + 1, jnp.int32)
        _lenS2 = 32 - jax.random.randint(jax.random.fold_in(_rk, 8), (128,), 0, max(1, 32 // 4) + 1, jnp.int32)
        cond_128 = 0.0061147 + 1.02565 * jax.random.normal(jax.random.fold_in(_rk, 11), (128, 128), jnp.float32)
        fside_S_0 = -0.022604 + 0.987366 * jax.random.normal(jax.random.fold_in(_rk, 12), (32,), jnp.float32)
        return (x, cond_128, fside_S_0)
    x, cond_128, fside_S_0 = _rec_inputs()

    def _L0_cond_setup():
        import jax, jax.numpy as jnp
        import numpy as np
        from jax import lax
        N, C_IN, L = (32, 32, 512)
        C_OUT, K, GROUPS = (32, 9, 4)
        C_DIM, PAD, STRIDE = (128, 4, 1)
        key = jax.random.key(seed)
        k1, k2, k3, k4, k5 = jax.random.split(key, 5)
        x = jax.random.normal(k1, (N, C_IN, L), dtype=jnp.float32)
        c = jax.random.normal(k2, (N, C_DIM), dtype=jnp.float32)
        weight = jax.random.normal(k3, (C_OUT, C_IN // GROUPS, K), dtype=jnp.float32)
        c_weight = jax.random.normal(k4, (C_OUT, C_DIM), dtype=jnp.float32)
        bias = jax.random.normal(k5, (C_OUT,), dtype=jnp.float32)
        return {'x': x, 'c': c, 'weight': weight, 'c_weight': c_weight, 'bias': bias}
    _L0_cond_all = _L0_cond_setup()
    _L0_cond_in = {k: v for k, v in _L0_cond_all.items() if k in ('weight', 'c_weight')}
    del _L0_cond_all

    def _L0_ffn_setup():
        import jax, jax.numpy as jnp
        import numpy as np
        D = 512
        F = 1376
        B, S = (4, 256)
        key = jax.random.key(seed)
        k_x, k_g, k_u, k_d = jax.random.split(key, 4)
        scale = 0.02
        return {'x': jax.random.normal(k_x, (B, S, D), dtype=jnp.float32), 'W_gate': jax.random.normal(k_g, (F, D), dtype=jnp.float32) * scale, 'W_up': jax.random.normal(k_u, (F, D), dtype=jnp.float32) * scale, 'W_down': jax.random.normal(k_d, (D, F), dtype=jnp.float32) * scale}
    _L0_ffn_all = _L0_ffn_setup()
    _L0_ffn_in = {k: v for k, v in _L0_ffn_all.items() if k in ('W_gate', 'W_up', 'W_down')}
    del _L0_ffn_all
    return {'x': x, 'cond_128': cond_128, 'fside_S_0': fside_S_0, 'L0_cond_weight': _L0_cond_in['weight'], 'L0_cond_c_weight': _L0_cond_in['c_weight'], 'L0_ffn_W_gate': _L0_ffn_in['W_gate'], 'L0_ffn_W_up': _L0_ffn_in['W_up'], 'L0_ffn_W_down': _L0_ffn_in['W_down']}

def reference(x, cond_128, fside_S_0, L0_cond_weight, L0_cond_c_weight, L0_ffn_W_gate, L0_ffn_W_up, L0_ffn_W_down):
    import jax
    import jax.numpy as jnp

    def _L0_cond_ref(x, c, weight, c_weight, bias):
        import jax, jax.numpy as jnp
        import numpy as np
        from jax import lax
        N, C_IN, L = (32, 32, 512)
        C_OUT, K, GROUPS = (32, 9, 4)
        C_DIM, PAD, STRIDE = (128, 4, 1)
        out = lax.conv_general_dilated(x, weight, window_strides=(STRIDE,), padding=[(PAD, PAD)], dimension_numbers=('NCH', 'OIH', 'NCH'), feature_group_count=GROUPS)
        ctx = jnp.einsum('nd,od->no', c, c_weight)
        out = out + ctx[:, :, None] + bias[None, :, None]
        return out

    def _L0_ffn_ref(x, W_gate, W_up, W_down):
        import jax, jax.numpy as jnp
        import numpy as np
        D = 512
        F = 1376
        B, S = (4, 256)
        out_shape = x.shape[:-1] + (W_down.shape[0],)
        xt = x.reshape(-1, x.shape[-1])
        up = xt @ W_up.T
        gate = jax.nn.silu(xt @ W_gate.T)
        y = gate * up @ W_down.T
        return y.reshape(out_shape)
    x = x + _L0_ffn_ref(_L0_cond_ref(x, cond_128, L0_cond_weight, L0_cond_c_weight, fside_S_0), L0_ffn_W_gate, L0_ffn_W_up, L0_ffn_W_down)
    return x

_drawn_inputs = setup_inputs


def setup_inputs(seed=0):
    import zlib

    import numpy as np

    out = dict(_drawn_inputs(seed))
    spreads = {}
    factors = {}
    for name, (base, spread) in spreads.items():
        noise = np.random.default_rng([zlib.crc32(name.encode()), seed]).standard_normal(out[name].shape)
        drawn = base * np.exp(spread * noise) if base else spread * noise
        out[name] = jnp.asarray(drawn.astype(out[name].dtype))
    for name, factor in factors.items():
        out[name] = (out[name] * factor).astype(out[name].dtype)
    return out
```

```python
from contextlib import ExitStack

import concourse.bass as bass
from concourse import mybir

F32 = mybir.dt.float32
F32R = mybir.dt.float32r
ALU = mybir.AluOpType
ACT = mybir.ActivationFunctionType

P = 128


def adaln_ffn(nc, x, cond, bias, conv_w, ctx_w, w_gate, w_up, w_down, out):
    N, CH, L = x.shape
    _, CG, TAPS = conv_w.shape
    F = w_gate.shape[0]
    G = CH // CG
    PAD = TAPS // 2
    R = P // CG
    KC = L // P
    JJ = P // R
    WB = 4
    STEPS = L // R // WB
    TOK = WB * P
    OB = TOK // N
    FC = -(-F // P)
    HEAD_P = R - PAD
    HEAD0 = HEAD_P * CG
    HALO = TAPS - 1
    QN = HALO + R
    TB0 = (R - HALO) * CG
    ROW = L + PAD
    assert N == P and CG == 8 and R == 16 and KC == 4 and QN % 2 == 0 and CH * CG * TAPS == conv_w.shape[0] * conv_w.shape[1] * conv_w.shape[2]

    def width(fc):
        return min(P, F - fc * P)

    GU_LOADS = -(-FC // 2)
    LOADS = 2 * GU_LOADS + KC
    GU_UNITS = 2 * FC
    D_PARTS = -(-FC // 4)
    UNITS = GU_UNITS + KC * D_PARTS
    UNITS_PER_STEP = 3
    NAT = max(2 * ROW, F)
    NSLOT = 3
    NPERM = 3

    def unit_load(u):
        if u < GU_UNITS:
            return (u // FC) * GU_LOADS + (u % FC) // 2
        return 2 * GU_LOADS + (u - GU_UNITS) // D_PARTS

    def last_unit(load):
        return max(u for u in range(UNITS) if unit_load(u) == load)

    def units_of(k):
        return range(UNITS_PER_STEP * k, min(UNITS_PER_STEP * (k + 1), UNITS))

    def loads_before(i):
        return sum(n < NSLOT or i >= 0 and last_unit(n - NSLOT) <= units_of(2 * i + 1)[-1] for n in range(LOADS))

    with ExitStack() as ctx:
        def sb(name, shape, dt=F32, stack=ctx):
            return stack.enter_context(nc.sbuf_tensor(name, shape, dt))

        def ps(name, shape):
            return ctx.enter_context(nc.psum_tensor(name, shape, F32))

        def sem(name):
            return ctx.enter_context(nc.semaphore(name))

        wgu_hi = sb("wgu_hi", [P, KC, 2, F], F32R)
        wgu_lo = sb("wgu_lo", [P, KC, 2, F], F32R)
        wd_hi = sb("wd_hi", [P, FC, L], F32R)
        wd_lo = sb("wd_lo", [P, FC, L], F32R)
        with ExitStack() as early:
            w_nat = sb("w_nat", [P, NSLOT, NAT], F32, early)
            w_perm = sb("w_perm", [P, NPERM, L], F32, early)
        h_hi = sb("h_hi", [P, KC, TOK], F32R)
        h_lo = sb("h_lo", [P, KC, TOK], F32R)
        g_hi = sb("g_hi", [P, 2, TOK], F32R)
        g_lo = sb("g_lo", [P, 2, TOK], F32R)
        stage = sb("stage", [P, 2, KC, TOK])
        x_in = sb("x_in", [P, CG, P])
        x_blk = sb("x_blk", [P, WB, R, CG])
        xt_hi = sb("xt_hi", [P, (2 * WB + 1) * P], F32R)
        xt_lo = sb("xt_lo", [P, (2 * WB + 1) * P], F32R)
        win = sb("win", [P, JJ, P])
        head = sb("head", [P, P])
        act_f = sb("act_f", [P, TOK])
        res = sb("res", [P, OB, L])
        ctxb = sb("ctxb", [P, G, P])
        toep = sb("toep", [P, G, QN, CG])
        ta_hi = sb("ta_hi", [P, P], F32R)
        ta_lo = sb("ta_lo", [P, P], F32R)
        tb_hi = sb("tb_hi", [P, P], F32R)
        tb_lo = sb("tb_lo", [P, P], F32R)
        ident = sb("ident", [P, P])

        ctx_w_rep = res[:, 0, :].rearrange("d (g p o) -> d g p o", g=G, p=R)
        cond_nat = res[:, 1, 0:P]
        cond_t = res[:, 1, P:2 * P]
        ctx_w_nat = res[0:CH, 1, 256:384]
        conv_w_t = res[0:CG * TAPS, 1, 384:384 + CH]
        conv_w_nat = res[0:CH, 1, 416:416 + CG * TAPS]
        SEL_W = QN + R - 1
        select = res[0:CG * TAPS, 2, 0:CG * SEL_W].rearrange("k (s c) -> k s c", c=CG)
        bias_nat = res[0:1, 2, 320:320 + CH]
        ones = res[0:1, 2, 352:352 + P]
        bias_rep = res[0:1, 3, :].rearrange("d (g p o) -> d g p o", g=G, p=R)

        acc = ps("acc", [P, OB, L])
        gate_ps = ps("gate_ps", [P, TOK])
        up_ps = ps("up_ps", [P, TOK])
        xt_ps = ps("xt_ps", [P, WB * P])
        conv_ps = ps("conv_ps", [P, WB * P])

        small_in = sem("small_in")
        consts = sem("consts")
        setup_t = sem("setup_t")
        setup_c = sem("setup_c")
        setup_mm = sem("setup_mm")
        setup_done = sem("setup_done")
        w_loaded = [sem(f"w_loaded{i}") for i in range(NSLOT)]
        w_wrapped = sem("w_wrapped")
        w_permuted = sem("w_permuted")
        w_turned = sem("w_turned")
        w_hi_done = sem("w_hi_done")
        acc_free = sem("acc_free")
        x_loaded = sem("x_loaded")
        blocking = sem("blocking")
        x_blocked = sem("x_blocked")
        x_turned = sem("x_turned")
        xt_hi_done = sem("xt_hi_done")
        xt_lo_done = sem("xt_lo_done")
        t_hi_done = sem("t_hi_done")
        t_lo_done = sem("t_lo_done")
        conv_done = sem("conv_done")
        conv_out = sem("conv_out")
        staged = [sem(f"staged{i}") for i in range(KC)]
        h_hi_done = sem("h_hi_done")
        h_lo_done = sem("h_lo_done")
        h_read = sem("h_read")
        gate_done = sem("gate_done")
        sig_done = sem("sig_done")
        silu_done = sem("silu_done")
        up_done = sem("up_done")
        g_done = sem("g_done")
        g_hi_done = sem("g_hi_done")
        g_lo_done = sem("g_lo_done")
        g_read = sem("g_read")
        y_done = sem("y_done")
        res_loaded = [sem(f"res_loaded{i}") for i in range(OB)]
        y_stored = [sem(f"y_stored{i}") for i in range(OB)]

        def weight_views(u, wgu, wd):
            bank = acc[:, u % OB, :].rearrange("p (i f) -> p i f", f=P)
            if u < GU_UNITS:
                which, fc = u // FC, u % FC
                w = width(fc)
                return [(wgu[:, :, which, fc * P:fc * P + w], bank[:, :, 0:w])]
            dq, part = (u - GU_UNITS) // D_PARTS, (u - GU_UNITS) % D_PARTS
            f0, f1 = 4 * part, min(4 * part + 4, F // P)
            views = [(wd[:, f0:f1, dq * P:(dq + 1) * P], bank[:, 0:f1 - f0, :])]
            if part == D_PARTS - 1 and F % P:
                views.append((wd[0:F % P, f1, dq * P:(dq + 1) * P], bank[0:F % P, f1 - f0, :]))
            return views

        CPG = STEPS + 1
        LD = 16

        def split3(hi_w, lo_w, hi_x, lo_x):
            return ((hi_w, hi_x), (lo_w, hi_x), (hi_w, lo_x))

        block = ctx.enter_context(nc.Block())

        @block.sync
        def _(sp):
            def load_x(grp, i):
                sp.dma_start(x_in[:], x[:, bass.ds(grp * CG, CG), i * P:(i + 1) * P]).then_inc(x_loaded, LD)

            def load_w(n):
                if n >= NSLOT + 2 * GU_LOADS:
                    sp.wait_ge(w_turned, last_unit(n - NSLOT) + 1)
                elif n >= NSLOT:
                    sp.wait_ge(w_permuted, last_unit(n - NSLOT) + 1)
                slot = w_nat[:, n % NSLOT, :]
                if n < 2 * GU_LOADS:
                    w, j = (w_gate, w_up)[n // GU_LOADS], n % GU_LOADS
                    rows = min(2 * P, F - 2 * P * j)
                    if rows == 2 * P:
                        dst = slot[:, 0:2 * ROW].rearrange("p (c l) -> p c l", c=2)[:, :, 0:L]
                        src = w[2 * P * j:2 * P * j + rows, :].rearrange("(c p) l -> p c l", p=P)
                    else:
                        dst, src = slot[0:rows, 0:L], w[2 * P * j:2 * P * j + rows, :]
                else:
                    dq = n - 2 * GU_LOADS
                    dst, src = slot[:, 0:F], w_down[dq * P:(dq + 1) * P, :]
                sp.dma_start(dst, src).then_inc(w_loaded[n % NSLOT], LD)

            def stage_chunk(grp, i):
                sp.wait_ge(conv_out, CPG * grp + 2 * i + 3)
                for o in range(CG):
                    sp.dma_start(stage[:, o // OB, i, (o % OB) * P:(o % OB + 1) * P],
                                 win[o:P:CG, :, :]).then_inc(staged[i], LD)

            def load_res(blk):
                for tt in range(OB):
                    sp.dma_start(res[:, tt, :], x[:, bass.ds(blk * OB + tt, 1), :]).then_inc(res_loaded[tt], LD)

            def store_y(blk, last=False):
                for tt in range(OB):
                    sp.wait_ge(acc_free, UNITS + OB * blk + tt + 1)
                    sp.dma_start(out[:, bass.ds(blk * OB + tt, 1), :], res[:, tt, :]).then_inc(y_stored[tt], LD)
                for tt in range(OB):
                    sp.wait_ge(y_stored[tt], LD * (blk + 1))
                if not last:
                    load_res(blk + 1)

            load_x(0, 0)
            for n in range(NSLOT):
                load_w(n)
            for i in range(KC):
                if i < KC - 1:
                    sp.wait_ge(x_blocked, 2 * i + 2)
                    load_x(0, i + 1)
                for n in range(loads_before(i - 1), loads_before(i)):
                    load_w(n)
                stage_chunk(0, i)
            for n in range(loads_before(KC - 1), LOADS):
                load_w(n)
            sp.wait_ge(setup_done, 2)
            load_res(0)

            def iteration(g, conv):
                if conv:
                    sp.wait_ge(x_blocked, STEPS * (g + 1))
                    load_x(g + 1, 0)
                store_y(2 * g)
                if conv:
                    for i in range(KC):
                        if i < KC - 1:
                            sp.wait_ge(x_blocked, STEPS * (g + 1) + 2 * i + 2)
                            load_x(g + 1, i + 1)
                        if i == 0:
                            sp.wait_ge(h_lo_done, 2 * KC * (g + 1))
                        stage_chunk(g + 1, i)
                store_y(2 * g + 1, last=not conv)

            with sp.Fori(0, G - 1) as g:
                iteration(g, True)
            iteration(G - 1, False)

        @block.gpsimd
        def _(pool):
            pool.memset(ident[:], 0.0).then_inc(consts, 1)
            pool.memset(res[0:CG * TAPS, 2, 0:CG * SEL_W], 0.0).then_inc(consts, 1)
            pool.memset(ones, 1.0).then_inc(consts, 1)
            pool.memset(tb_hi[:, 0:TB0].bitcast(F32), 0.0).then_inc(consts, 1)
            pool.memset(tb_lo[:, 0:TB0].bitcast(F32), 0.0).then_inc(consts, 1)
            pool.wait_ge(consts, 5)
            pool.affine_select(out=ident[:], in_=ident[:], compare_op=ALU.not_equal, fill=1.0, base=0,
                               pattern=[[-1, P]], channel_multiplier=1).then_inc(consts, 1)
            sel = select[:, R - 1:R - 1 + TAPS, :]
            pool.affine_select(out=sel, in_=sel, compare_op=ALU.not_equal, fill=1.0, base=0,
                               pattern=[[-1, TAPS], [-TAPS, CG]], channel_multiplier=1).then_inc(consts, 1)

            def block_x(grp, k):
                if k % 2 == 0:
                    pool.wait_ge(x_loaded, LD * (KC * grp + k // 2 + 1))
                if not (isinstance(grp, int) and k == 0):
                    pool.wait_ge(x_turned, STEPS * grp + k)
                pool.sem_inc(blocking, 1)
                r0 = (k % 2) * WB * R
                pool.tensor_copy(x_blk[:], x_in[:, :, r0:r0 + WB * R].rearrange("n c (b r) -> n b r c", r=R)
                                 ).then_inc(x_blocked, 1)

            def permute_w(u):
                n, fc = unit_load(u), u % FC
                w, c = width(fc), fc % 2
                row = w_nat[0:w, n % NSLOT, c * ROW:(c + 1) * ROW]
                if c == 0:
                    pool.wait_ge(w_loaded[n % NSLOT], LD * (n // NSLOT + 1))
                pool.tensor_copy(row[:, L:ROW], row[:, 0:PAD]).then_inc(w_wrapped, 1)
                pool.wait_ge(w_wrapped, u + 1)
                if u >= NPERM:
                    pool.wait_ge(w_turned, u - NPERM + 1)
                pool.tensor_copy(w_perm[0:w, u % NPERM, :].rearrange("f (i p j) -> f i p j", i=KC, p=R),
                                 row[:, PAD:ROW].rearrange("f (i j p) -> f i p j", i=KC, p=R)).then_inc(w_permuted, 1)

            block_x(0, 0)
            for k in range(STEPS):
                if k < STEPS - 1:
                    block_x(0, k + 1)
                for u in units_of(k):
                    if u < GU_UNITS:
                        permute_w(u)
            with pool.Fori(0, G - 1) as g:
                for k in range(STEPS):
                    block_x(g + 1, k)

        @block.tensor
        def _(pe):
            def setup():
                pe.wait_ge(consts, 7)
                pe.wait_ge(small_in, 4 * LD)
                pe.transpose(xt_ps[0:CG * TAPS, 0:CH], conv_w_nat, ident[0:CH, 0:CH])
                pe.transpose(xt_ps[:, P:P + CH], ctx_w_nat, ident[0:CH, 0:CH])
                pe.transpose(xt_ps[:, 2 * P:3 * P], cond_nat, ident[:]).then_inc(setup_t, 1)
                pe.wait_ge(setup_c, 1)
                for q in range(QN):
                    bank, at = (gate_ps, up_ps)[q // (QN // 2)], (q % (QN // 2)) * CH
                    first = QN - 1 - q
                    mm = pe.matmul(bank[:, at:at + CH], select[:, first:first + R, :], conv_w_t, start=True, stop=True)
                mm.then_inc(setup_mm, 1)
                for g in range(G):
                    pe.matmul(conv_ps[:, g * P:(g + 1) * P], ctx_w_rep[:, g, :, :], cond_t, start=True, stop=False)
                    mm = pe.matmul(conv_ps[:, g * P:(g + 1) * P], bias_rep[:, g, :, :], ones, start=False, stop=True)
                mm.then_inc(setup_mm, 1)

            def turn_x(grp, k):
                pe.wait_ge(x_blocked, STEPS * grp + k + 1)
                if not (isinstance(grp, int) and grp == 0 and k == 0):
                    pe.wait_ge(xt_lo_done, STEPS * grp + k)
                for b in range(WB):
                    mm = pe.transpose(xt_ps[:, b * P:(b + 1) * P], x_blk[:, b, :, :], ident[:])
                mm.then_inc(x_turned, 1)

            def conv_head(grp):
                pe.wait_ge(t_lo_done, grp + 1)
                pe.wait_ge(xt_lo_done, STEPS * grp + 1)
                if isinstance(grp, int):
                    pe.wait_ge(setup_done, 2)
                else:
                    pe.wait_ge(conv_out, CPG * grp)
                passes = split3(tb_hi, tb_lo, xt_hi, xt_lo)
                for n, (t, v) in enumerate(passes):
                    mm = pe.matmul(conv_ps[:, 0:P], t[:], v[:, 0:P], start=n == 0, stop=n == 2)
                mm.then_inc(conv_done, 1)

            def conv_step(grp, k):
                pe.wait_ge(xt_lo_done, STEPS * grp + min(k + 2, STEPS))
                pe.wait_ge(conv_out, CPG * grp + k + 1)
                at = (k % 2) * WB * P
                for n, (t, v) in enumerate(split3(ta_hi, ta_lo, xt_hi, xt_lo)):
                    pe.matmul(conv_ps[:], t[:], v[:, at:at + WB * P], start=n == 0, stop=False)
                cols = (WB if k < STEPS - 1 else WB - 1) * P
                for n, (t, v) in enumerate(split3(tb_hi, tb_lo, xt_hi, xt_lo)):
                    mm = pe.matmul(conv_ps[:, 0:cols], t[:], v[:, at + P:at + P + cols], start=False, stop=n == 2)
                mm.then_inc(conv_done, 1)

            def turn_w(u):
                n = unit_load(u)
                slot = w_nat[:, n % NSLOT, :]
                if u >= OB:
                    pe.wait_ge(acc_free, u - OB + 1)
                if u < GU_UNITS:
                    pe.wait_ge(w_permuted, u + 1)
                    fc = u % FC
                    w = width(fc)
                    for i in range(KC):
                        mm = pe.transpose(acc[:, u % OB, i * P:i * P + w], w_perm[0:w, u % NPERM, i * P:(i + 1) * P],
                                          ident[0:w, 0:w])
                else:
                    pe.wait_ge(w_loaded[n % NSLOT], LD * (n // NSLOT + 1))
                    part = (u - GU_UNITS) % D_PARTS
                    for s, fc in enumerate(range(4 * part, min(4 * part + 4, FC))):
                        w = width(fc)
                        mm = pe.transpose(acc[0:w, u % OB, s * P:(s + 1) * P], slot[:, fc * P:fc * P + w], ident[:])
                mm.then_inc(w_turned, 1)

            def product(bank, which, f, fresh_at=None, last_read=False, mark_first=False):
                w = width(f)
                for i in range(KC):
                    if fresh_at is not None:
                        pe.wait_ge(h_lo_done, fresh_at + i + 1)
                    for n, (wt, hv) in enumerate(split3(wgu_hi, wgu_lo, h_hi, h_lo)):
                        mm = pe.matmul(bank[0:w, :], wt[:, i, which, f * P:f * P + w], hv[:, i, :],
                                       start=i == 0 and n == 0, stop=i == KC - 1 and n == 2)
                        if mark_first and i == 0 and n == 0:
                            mm.then_inc(g_read, 1)
                    if last_read and i < KC - 1:
                        mm.then_inc(h_read, 1)
                return mm

            def down(t, blk, half, f):
                pe.wait_ge(g_lo_done, t + 1)
                w = width(f)
                for tt in range(OB):
                    if f == 0:
                        pe.wait_ge(acc_free, UNITS - OB + OB * blk + tt + 1)
                    at = slice(tt * P, (tt + 1) * P)
                    for n, (gs, wt) in enumerate(((g_hi, wd_hi), (g_hi, wd_lo), (g_lo, wd_hi))):
                        mm = pe.matmul(acc[:, tt, :], gs[0:w, (half * FC + f) % 2, at], wt[0:w, f, :], start=f == 0 and n == 0, stop=f == FC - 1 and n == 2)
                    if f == FC - 1 and tt < OB - 1:
                        mm.then_inc(y_done, 1)
                mm.then_inc(g_read, 1)

            setup()
            turn_x(0, 0)
            for k in range(STEPS):
                if k < STEPS - 1:
                    turn_x(0, k + 1)
                for u in units_of(k):
                    turn_w(u)
                if k == 0:
                    conv_head(0)
                conv_step(0, k)
            for u in range(UNITS_PER_STEP * STEPS, UNITS):
                turn_w(u)
            pe.wait_ge(acc_free, UNITS)
            product(gate_ps, 0, 0, fresh_at=0).then_inc(gate_done, 1)
            product(up_ps, 1, 0, mark_first=True).then_inc(up_done, 1)

            def iteration(g, conv):
                for half in range(2):
                    blk = 2 * g + half
                    for f in range(FC):
                        t = blk * FC + f
                        nf = (f + 1) % FC
                        more = conv or half == 0 or f < FC - 1
                        if more:
                            pe.wait_ge(silu_done, t + 1)
                            product(gate_ps, 0, nf, fresh_at=KC * (blk + 1) if nf == 0 else None).then_inc(gate_done, 1)
                        if conv and half == 1 and f < STEPS:
                            turn_x(g + 1, f)
                        if more:
                            pe.wait_ge(g_done, t + 1)
                            product(up_ps, 1, nf, last_read=nf == FC - 1).then_inc(up_done, 1)
                        if conv and half == 1 and f == 0:
                            conv_head(g + 1)
                        if conv and half == 1 and 1 <= f <= STEPS:
                            conv_step(g + 1, f - 1)
                        down(t, blk, half, f)

            with pe.Fori(0, G - 1) as g:
                iteration(g, True)
            iteration(G - 1, False)

        @block.scalar
        def _(act):
            def hi(dst, src):
                return act.activation(dst, src, ACT.Copy)

            def split_toep(grp):
                if isinstance(grp, int):
                    act.wait_ge(setup_done, 1)
                else:
                    act.wait_ge(conv_done, CPG * grp)
                hi(ta_hi[:], toep[:, bass.ds(grp, 1), HALO:QN, :])
                hi(tb_hi[:, TB0:P], toep[:, bass.ds(grp, 1), 0:HALO, :]).then_inc(t_hi_done, 1)

            def split_x(grp, k):
                if k >= 2:
                    act.wait_ge(conv_done, CPG * grp + k)
                elif not isinstance(grp, int):
                    act.wait_ge(conv_done, CPG * grp)
                act.wait_ge(x_turned, STEPS * grp + k + 1)
                at = (k % 2) * WB * P
                last = hi(xt_hi[:, at:at + WB * P], xt_ps[:])
                if k % 2 == 0 and k > 0:
                    last = hi(xt_hi[:, 2 * WB * P:], xt_ps[:, 0:P])
                last.then_inc(xt_hi_done, 1)

            def split_w(u):
                act.wait_ge(w_turned, u + 1)
                for dst, src in weight_views(u, wgu_hi, wd_hi):
                    last = hi(dst, src)
                last.then_inc(w_hi_done, 1)

            def split_h(grp, half, first=False):
                blk = 2 * grp + half
                for i in range(KC):
                    act.wait_ge(staged[i], LD * CG * (grp + 1))
                    if first:
                        act.wait_ge(w_turned, UNITS)
                    elif i < KC - 1:
                        act.wait_ge(h_read, (KC - 1) * (blk - 1) + i + 1)
                    else:
                        act.wait_ge(up_done, FC * blk)
                    hi(h_hi[:, i, :], stage[:, half, i, :]).then_inc(h_hi_done, 1)

            def sigmoid(s, f, first=False):
                act.wait_ge(gate_done, s + 1)
                if not first:
                    act.wait_ge(g_lo_done, s)
                w = width(f)
                act.activation(act_f[0:w, :], gate_ps[0:w, :], ACT.Sigmoid).then_inc(sig_done, 1)

            def split_g(s, f, slot, first=False):
                act.wait_ge(g_done, s + 1)
                if not first:
                    act.wait_ge(g_read, s)
                w = width(f)
                hi(g_hi[0:w, slot, :], act_f[0:w, :]).then_inc(g_hi_done, 1)

            act.dma_start(conv_w_nat, conv_w.rearrange("o c k -> o (c k)")).then_inc(small_in, LD)
            act.dma_start(ctx_w_nat, ctx_w).then_inc(small_in, LD)
            act.dma_start(cond_nat, cond).then_inc(small_in, LD)
            act.dma_start(bias_nat, bias.rearrange("(a o) -> a o", a=1)).then_inc(small_in, LD)
            split_toep(0)
            split_x(0, 0)
            for k in range(STEPS):
                if k < STEPS - 1:
                    split_x(0, k + 1)
                for u in units_of(k):
                    split_w(u)
            for u in range(UNITS_PER_STEP * STEPS, UNITS):
                split_w(u)
            split_h(0, 0, first=True)
            sigmoid(0, 0, first=True)
            split_g(0, 0, 0, first=True)

            def iteration(g, conv):
                for half in range(2):
                    for f in range(FC):
                        s, nf = (2 * g + half) * FC + f + 1, (f + 1) % FC
                        if conv or half == 0 or f < FC - 1:
                            sigmoid(s, nf)
                            if conv and half == 0 and f == 0:
                                split_toep(g + 1)
                            if conv and half == 1 and f < STEPS:
                                split_x(g + 1, f)
                            if nf == FC - 1 and half == 0:
                                split_h(g, 1)
                            if nf == FC - 1 and half == 1 and conv:
                                split_h(g + 1, 0)
                            split_g(s, nf, (half * FC + f + 1) % 2)

            with act.Fori(0, G - 1) as g:
                iteration(g, True)
            iteration(G - 1, False)

        @block.vector
        def _(dve):
            def lo(dst, src, hi_part):
                return dve.tensor_tensor(dst, src, hi_part.bitcast(F32), ALU.subtract)

            def setup():
                dve.wait_ge(setup_t, 1)
                dve.tensor_copy(conv_w_t, xt_ps[0:CG * TAPS, 0:CH])
                dve.tensor_copy(cond_t, xt_ps[:, 2 * P:3 * P])
                dve.tensor_copy(ctx_w_rep, xt_ps[:, P:P + CH].rearrange("d (g a o) -> d g a o", g=G, a=1)
                                .broadcast_to([P, G, R, CG]))
                dve.wait_ge(small_in, 4 * LD)
                dve.tensor_copy(bias_rep, bias_nat.rearrange("d (g a o) -> d g a o", g=G, a=1)
                                .broadcast_to([1, G, R, CG])).then_inc(setup_c, 1)
                dve.wait_ge(setup_mm, 1)
                for n, bank in enumerate((gate_ps, up_ps)):
                    q0 = n * (QN // 2)
                    last = dve.tensor_copy(toep[:, :, q0:q0 + QN // 2, :],
                                           bank[:, 0:QN // 2 * CH].rearrange("p (q g o) -> p g q o", g=G, o=CG))
                last.then_inc(setup_done, 1)
                dve.wait_ge(setup_mm, 2)
                dve.tensor_copy(ctxb[:].rearrange("p g n -> p (g n)"), conv_ps[:]).then_inc(setup_done, 1)

            def split_toep(grp):
                if isinstance(grp, int):
                    dve.wait_ge(setup_done, 2)
                dve.wait_ge(t_hi_done, grp + 1)
                lo(ta_lo[:].rearrange("p (q o) -> p q o", o=CG), toep[:, bass.ds(grp, 1), HALO:QN, :],
                   ta_hi[:].rearrange("p (q o) -> p q o", o=CG))
                lo(tb_lo[:, TB0:P], toep[:, bass.ds(grp, 1), 0:HALO, :], tb_hi[:, TB0:P]).then_inc(t_lo_done, 1)

            def split_x(grp, k):
                dve.wait_ge(xt_hi_done, STEPS * grp + k + 1)
                at = (k % 2) * WB * P
                last = lo(xt_lo[:, at:at + WB * P], xt_ps[:], xt_hi[:, at:at + WB * P])
                if k % 2 == 0 and k > 0:
                    last = lo(xt_lo[:, 2 * WB * P:], xt_ps[:, 0:P], xt_hi[:, 2 * WB * P:])
                last.then_inc(xt_lo_done, 1)

            def split_w(u):
                dve.wait_ge(w_hi_done, u + 1)
                for (dst, src), (hi_part, _) in zip(weight_views(u, wgu_lo, wd_lo), weight_views(u, wgu_hi, wd_hi)):
                    last = lo(dst, src, hi_part)
                last.then_inc(acc_free, 1)

            def read_head(grp):
                dve.wait_ge(conv_done, CPG * grp + 1)
                dve.tensor_tensor(head[HEAD0:P, :], conv_ps[HEAD0:P, 0:P], ctxb[HEAD0:P, bass.ds(grp, 1), :],
                                  ALU.add).then_inc(conv_out, 1)

            def read_conv(grp, k):
                i = k // 2
                if k % 2 == 0 and i > 0:
                    dve.wait_ge(staged[i - 1], LD * CG * (grp + 1))
                elif k % 2 == 0 and not isinstance(grp, int):
                    dve.wait_ge(staged[KC - 1], LD * CG * grp)
                dve.wait_ge(conv_done, CPG * grp + k + 2)
                w0, n = (k % 2) * WB, WB if k < STEPS - 1 else WB - 1
                last = dve.tensor_tensor(win[:, w0:w0 + n, :], conv_ps[:, 0:n * P].rearrange("p (w n) -> p w n", w=n),
                                         ctxb[:, bass.ds(grp, 1), :].broadcast_to([P, n, P]), ALU.add)
                if k == STEPS - 1:
                    dve.tensor_tensor(win[0:HEAD0, JJ - 1, :], conv_ps[0:HEAD0, n * P:(n + 1) * P],
                                      ctxb[0:HEAD0, bass.ds(grp, 1), :], ALU.add)
                    dve.wait_ge(conv_out, CPG * grp + 1)
                    last = dve.tensor_copy(win[HEAD0:P, JJ - 1, :], head[HEAD0:P, :])
                last.then_inc(conv_out, 1)

            def split_h(blk, half):
                for i in range(KC):
                    dve.wait_ge(h_hi_done, KC * blk + i + 1)
                    lo(h_lo[:, i, :], stage[:, half, i, :], h_hi[:, i, :]).then_inc(h_lo_done, 1)

            def silu(s, f):
                dve.wait_ge(sig_done, s + 1)
                w = width(f)
                dve.tensor_tensor(act_f[0:w, :], gate_ps[0:w, :], act_f[0:w, :], ALU.mult).then_inc(silu_done, 1)

            def gated(s, f):
                dve.wait_ge(up_done, s + 1)
                dve.wait_ge(silu_done, s + 1)
                w = width(f)
                dve.tensor_tensor(act_f[0:w, :], up_ps[0:w, :], act_f[0:w, :], ALU.mult).then_inc(g_done, 1)

            def split_g(s, f, slot):
                dve.wait_ge(g_hi_done, s + 1)
                w = width(f)
                lo(g_lo[0:w, slot, :], act_f[0:w, :], g_hi[0:w, slot, :]).then_inc(g_lo_done, 1)

            def add_residual(blk):
                for tt in range(OB):
                    dve.wait_ge(res_loaded[tt], LD * (blk + 1))
                    if tt < OB - 1:
                        dve.wait_ge(y_done, (OB - 1) * blk + tt + 1)
                    else:
                        dve.wait_ge(g_read, FC * (blk + 1) + 1)
                    dve.tensor_tensor(res[:, tt, :], acc[:, tt, :], res[:, tt, :], ALU.add).then_inc(acc_free, 1)

            setup()
            split_toep(0)
            split_x(0, 0)
            for k in range(STEPS):
                if k < STEPS - 1:
                    split_x(0, k + 1)
                for u in units_of(k):
                    split_w(u)
                if k == 0:
                    read_head(0)
                read_conv(0, k)
            for u in range(UNITS_PER_STEP * STEPS, UNITS):
                split_w(u)
            split_h(0, 0)
            silu(0, 0)
            gated(0, 0)
            split_g(0, 0, 0)

            def iteration(g, conv):
                for half in range(2):
                    blk = 2 * g + half
                    for f in range(FC):
                        s, nf = blk * FC + f + 1, (f + 1) % FC
                        if conv or half == 0 or f < FC - 1:
                            silu(s, nf)
                            if conv and half == 0 and f == 0:
                                split_toep(g + 1)
                            if conv and half == 1 and f < STEPS:
                                split_x(g + 1, f)
                            if nf == FC - 1 and (half == 0 or conv):
                                split_h(blk + 1, 1 - half)
                            gated(s, nf)
                            if conv and half == 1 and f == 0:
                                read_head(g + 1)
                            if conv and half == 1 and 1 <= f <= STEPS:
                                read_conv(g + 1, f - 1)
                            split_g(s, nf, (half * FC + f + 1) % 2)
                    add_residual(blk)

            with dve.Fori(0, G - 1) as g:
                iteration(g, True)
            iteration(G - 1, False)


_INS = ["x", "cond_128", "fside_S_0", "L0_cond_weight", "L0_cond_c_weight", "L0_ffn_W_gate", "L0_ffn_W_up", "L0_ffn_W_down"]


def kernel(**inputs):
    import numpy as np
    import concourse.bacc as bacc
    from concourse.bass_utils import run_bass_kernel_spmd

    nc = bacc.Bacc("TRN2", target_bir_lowering=False, num_devices=1)
    arrays, args = {}, []
    for name in _INS:
        a = np.ascontiguousarray(inputs[name])
        arrays[f"in_{name}"] = a
        args.append(nc.dram_tensor(f"in_{name}", a.shape, mybir.dt.from_np(a.dtype), kind="ExternalInput").ap())
    args.append(nc.dram_tensor("out_y", inputs["x"].shape, F32, kind="ExternalOutput").ap())
    adaln_ffn(nc, *args)
    r = run_bass_kernel_spmd(nc, [arrays], core_ids=[0])
    return r.results[0]["out_y"]
```

```python
from contextlib import ExitStack

import concourse.bass as bass
from concourse import mybir

F32 = mybir.dt.float32
F32R = mybir.dt.float32r
BF16 = mybir.dt.bfloat16
ALU = mybir.AluOpType
ACT = mybir.ActivationFunctionType

P = 128


def adaln_ffn(nc, x, cond, bias, conv_w, ctx_w, w_gate, w_up, w_down, out):
    N, CH, L = x.shape
    _, CG, TAPS = conv_w.shape
    F = w_gate.shape[0]
    G = CH // CG
    PAD = TAPS // 2
    R = P // CG
    KC = L // P
    JJ = P // R
    WB = 4
    STEPS = L // R // WB
    TOK = WB * P
    OB = TOK // N
    FC = -(-F // P)
    HEAD_P = R - PAD
    HEAD0 = HEAD_P * CG
    HALO = TAPS - 1
    QN = HALO + R
    TB0 = (R - HALO) * CG
    ROW = L + PAD
    assert N == P and CG == 8 and R == 16 and KC == 4 and QN % 2 == 0 and CH * CG * TAPS == conv_w.shape[0] * conv_w.shape[1] * conv_w.shape[2]

    def width(fc):
        return min(P, F - fc * P)

    GU_LOADS = -(-FC // 2)
    LOADS = 2 * GU_LOADS + KC
    GU_UNITS = 2 * FC
    D_PARTS = -(-FC // 4)
    UNITS = GU_UNITS + KC * D_PARTS
    UNITS_PER_STEP = 3
    NAT = max(2 * ROW, F)
    NSLOT = 3
    NPERM = 3
    PERM_AHEAD = 2

    def unit_load(u):
        if u < GU_UNITS:
            return (u // FC) * GU_LOADS + (u % FC) // 2
        return 2 * GU_LOADS + (u - GU_UNITS) // D_PARTS

    def last_unit(load):
        return max(u for u in range(UNITS) if unit_load(u) == load)

    def permuter(u):
        return ("ACT", "ACT", "ACT", "POOL")[u % 4]

    def permuted(u):
        return sum(permuter(v) == permuter(u) for v in range(u + 1))

    def units_of(k):
        return range(UNITS_PER_STEP * k, min(UNITS_PER_STEP * (k + 1), UNITS))

    with ExitStack() as ctx:
        def sb(name, shape, dt=F32, stack=ctx):
            return stack.enter_context(nc.sbuf_tensor(name, shape, dt))

        def ps(name, shape):
            return ctx.enter_context(nc.psum_tensor(name, shape, F32))

        def sem(name):
            return ctx.enter_context(nc.semaphore(name))

        wgu_hi = sb("wgu_hi", [P, KC, 2, F], F32R)
        wgu_lo = sb("wgu_lo", [P, KC, 2, F], F32R)
        wd_hi = sb("wd_hi", [P, FC, L], F32R)
        wd_lo = sb("wd_lo", [P, FC, L], F32R)
        with ExitStack() as early:
            w_nat = sb("w_nat", [P, NSLOT, NAT], F32, early)
            w_perm = sb("w_perm", [P, NPERM, L], F32, early)
        h_hi = sb("h_hi", [P, KC, TOK], F32R)
        h_lo = sb("h_lo", [P, KC, TOK], F32R)
        g_hi = sb("g_hi", [P, 2, TOK], F32R)
        g_lo = sb("g_lo", [P, 2, TOK], F32R)
        stage = sb("stage", [P, 2, KC, TOK])
        x_in = sb("x_in", [P, CG, P])
        x_blk = sb("x_blk", [P, WB, R, CG])
        xt_hi = sb("xt_hi", [P, (2 * WB + 1) * P], F32R)
        xt_lo = sb("xt_lo", [P, (2 * WB + 1) * P], F32R)
        win = sb("win", [P, JJ, P])
        head = sb("head", [P, P])
        act_f = sb("act_f", [P, TOK])
        res = sb("res", [P, OB, L])
        ctxb = sb("ctxb", [P, G, P])
        toep = sb("toep", [P, G, QN, CG])
        ta_hi = sb("ta_hi", [P, P], F32R)
        ta_lo = sb("ta_lo", [P, P], F32R)
        tb_hi = sb("tb_hi", [P, P], F32R)
        tb_lo = sb("tb_lo", [P, P], F32R)
        ident = sb("ident", [P, P])

        ctx_w_rep = res[:, 0, :].rearrange("d (g p o) -> d g p o", g=G, p=R)
        cond_nat = res[:, 1, 0:P]
        cond_t = res[:, 1, P:2 * P]
        ctx_w_nat = res[0:CH, 1, 256:384]
        conv_w_t = res[0:CG * TAPS, 1, 384:384 + 3 * CH // 2].bitcast(BF16).rearrange("k (a o) -> k a o", a=3)
        conv_w_nat = res[0:CH, 1, 432:432 + CG * TAPS]
        conv_w_rest = res[0:CG * TAPS, 2, 160:160 + 2 * CH].rearrange("k (a o) -> k a o", a=2)
        SEL_W = QN + R - 1
        select = res[0:CG * TAPS, 2, 0:CG * SEL_W // 2].bitcast(BF16).rearrange("k (s c) -> k s c", c=CG)
        bias_nat = res[0:1, 2, 320:320 + CH]
        ones = res[0:1, 2, 352:352 + P]
        bias_rep = res[0:1, 3, :].rearrange("d (g p o) -> d g p o", g=G, p=R)

        acc = ps("acc", [P, OB, L])
        gate_ps = ps("gate_ps", [P, TOK])
        up_ps = ps("up_ps", [P, TOK])
        xt_ps = ps("xt_ps", [P, WB * P])
        conv_ps = ps("conv_ps", [P, WB * P])

        small_in = sem("small_in")
        consts = sem("consts")
        setup_t = sem("setup_t")
        parts = sem("parts")
        setup_c = sem("setup_c")
        setup_mm = sem("setup_mm")
        setup_done = sem("setup_done")
        w_loaded = [sem(f"w_loaded{i}") for i in range(NSLOT)]
        w_wrapped = sem("w_wrapped")
        w_permuted = {e: sem(f"w_permuted_{e}") for e in ("ACT", "POOL")}
        w_turned = sem("w_turned")
        w_hi_done = sem("w_hi_done")
        acc_free = sem("acc_free")
        x_loaded = sem("x_loaded")
        blocking = sem("blocking")
        x_blocked = sem("x_blocked")
        x_turned = sem("x_turned")
        xt_hi_done = sem("xt_hi_done")
        xt_lo_done = sem("xt_lo_done")
        t_hi_done = sem("t_hi_done")
        t_lo_done = sem("t_lo_done")
        conv_done = sem("conv_done")
        conv_out = sem("conv_out")
        staged = [sem(f"staged{i}") for i in range(KC)]
        h_hi_done = sem("h_hi_done")
        h_lo_done = sem("h_lo_done")
        h_read = sem("h_read")
        gate_done = sem("gate_done")
        sig_done = sem("sig_done")
        silu_done = sem("silu_done")
        up_done = sem("up_done")
        g_done = sem("g_done")
        g_hi_done = sem("g_hi_done")
        g_lo_done = sem("g_lo_done")
        g_read = sem("g_read")
        y_done = sem("y_done")
        res_loaded = [sem(f"res_loaded{i}") for i in range(OB)]
        y_stored = [sem(f"y_stored{i}") for i in range(OB)]

        def weight_views(u, wgu, wd):
            bank = acc[:, u % OB, :].rearrange("p (i f) -> p i f", f=P)
            if u < GU_UNITS:
                which, fc = u // FC, u % FC
                w = width(fc)
                return [(wgu[:, :, which, fc * P:fc * P + w], bank[:, :, 0:w])]
            dq, part = (u - GU_UNITS) // D_PARTS, (u - GU_UNITS) % D_PARTS
            f0, f1 = 4 * part, min(4 * part + 4, F // P)
            views = [(wd[:, f0:f1, dq * P:(dq + 1) * P], bank[:, 0:f1 - f0, :])]
            if part == D_PARTS - 1 and F % P:
                views.append((wd[0:F % P, f1, dq * P:(dq + 1) * P], bank[0:F % P, f1 - f0, :]))
            return views

        CPG = STEPS + 1
        LD = 16

        def split3(hi_w, lo_w, hi_x, lo_x):
            return ((hi_w, hi_x), (lo_w, hi_x), (hi_w, lo_x))

        def copy_block(eng, k):
            r0 = (k % 2) * WB * R
            eng.tensor_copy(x_blk[:], x_in[:, :, r0:r0 + WB * R].rearrange("n c (b r) -> n b r c", r=R)
                            ).then_inc(x_blocked, 1)

        def load_x(eng, grp, i):
            eng.dma_start(x_in[:], x[:, bass.ds(grp * CG, CG), i * P:(i + 1) * P]).then_inc(x_loaded, LD)

        def permute_w(eng, copy, u):
            n, w, at = unit_load(u), width(u % FC), (u % FC) % 2 * ROW + PAD
            eng.wait_ge(w_wrapped, n + 1)
            if u >= NPERM:
                eng.wait_ge(w_turned, u - NPERM + 1)
            copy(w_perm[0:w, u % NPERM, :].rearrange("f (i p j) -> f i p j", i=KC, p=R),
                 w_nat[0:w, n % NSLOT, at:at + L].rearrange("f (i j p) -> f i p j", i=KC, p=R)
                 ).then_inc(w_permuted[permuter(u)], 1)

        def load_w(eng, n):
            if n >= NSLOT:
                eng.wait_ge(w_turned, last_unit(n - NSLOT) + 1)
            slot = w_nat[:, n % NSLOT, :]
            if n < 2 * GU_LOADS:
                w, j = (w_gate, w_up)[n // GU_LOADS], n % GU_LOADS
                rows = min(2 * P, F - 2 * P * j)
                if rows == 2 * P:
                    dst = slot[:, 0:2 * ROW].rearrange("p (c l) -> p c l", c=2)[:, :, 0:L]
                    src = w[2 * P * j:2 * P * j + rows, :].rearrange("(c p) l -> p c l", p=P)
                else:
                    dst, src = slot[0:rows, 0:L], w[2 * P * j:2 * P * j + rows, :]
            else:
                dq = n - 2 * GU_LOADS
                dst, src = slot[:, 0:F], w_down[dq * P:(dq + 1) * P, :]
            eng.dma_start(dst, src).then_inc(w_loaded[n % NSLOT], LD)

        def windows(grp, i):
            if isinstance(grp, int) and i in (1, 2):
                return res[:, 2 * i - 2:2 * i, :].rearrange("p a (w n) -> p (a w) n", n=P)
            return win

        block = ctx.enter_context(nc.Block())

        @block.sync
        def _(sp):
            def stage_chunk(grp, i):
                sp.wait_ge(conv_out, CPG * grp + 2 * i + 3)
                for o in range(CG):
                    sp.dma_start(stage[:, o // OB, i, (o % OB) * P:(o % OB + 1) * P],
                                 windows(grp, i)[o:P:CG, :, :]).then_inc(staged[i], LD)

            def load_res(blk):
                for tt in range(OB):
                    sp.dma_start(res[:, tt, :], x[:, bass.ds(blk * OB + tt, 1), :]).then_inc(res_loaded[tt], LD)

            def store_y(blk, last=False):
                for tt in range(OB):
                    sp.wait_ge(acc_free, UNITS + OB * blk + tt + 1)
                    sp.dma_start(out[:, bass.ds(blk * OB + tt, 1), :], res[:, tt, :]).then_inc(y_stored[tt], LD)
                for tt in range(OB):
                    sp.wait_ge(y_stored[tt], LD * (blk + 1))
                if not last:
                    load_res(blk + 1)

            sp.dma_start(conv_w_nat, conv_w.rearrange("o c k -> o (c k)")).then_inc(small_in, LD)
            sp.dma_start(ctx_w_nat, ctx_w).then_inc(small_in, LD)
            sp.dma_start(cond_nat, cond).then_inc(small_in, LD)
            sp.dma_start(bias_nat, bias.rearrange("(a o) -> a o", a=1)).then_inc(small_in, LD)
            load_x(sp, 0, 0)
            for n in range(NSLOT):
                load_w(sp, n)
            for i in range(KC):
                stage_chunk(0, i)
            for i in (1, 2):
                sp.wait_ge(staged[i], LD * CG)
            load_res(0)

            def iteration(g, conv):
                if conv:
                    sp.wait_ge(x_blocked, STEPS * (g + 1))
                    load_x(sp, g + 1, 0)
                store_y(2 * g)
                if conv:
                    for i in range(KC):
                        if i < KC - 1:
                            sp.wait_ge(x_blocked, STEPS * (g + 1) + 2 * i + 2)
                            load_x(sp, g + 1, i + 1)
                        if i == 0:
                            sp.wait_ge(h_lo_done, 2 * KC * (g + 1))
                        stage_chunk(g + 1, i)
                store_y(2 * g + 1, last=not conv)

            with sp.Fori(0, G - 1) as g:
                iteration(g, True)
            iteration(G - 1, False)

        @block.gpsimd
        def _(pool):
            pool.memset(ident[:], 0.0).then_inc(consts, 1)
            pool.memset(res[0:CG * TAPS, 2, 0:CG * SEL_W // 2], 0.0).then_inc(consts, 1)
            pool.memset(ones, 1.0).then_inc(consts, 1)
            pool.memset(tb_hi[:, 0:TB0].bitcast(F32), 0.0).then_inc(consts, 1)
            pool.memset(tb_lo[:, 0:TB0].bitcast(F32), 0.0).then_inc(consts, 1)
            pool.wait_ge(consts, 5)
            pool.affine_select(out=ident[:], in_=ident[:], compare_op=ALU.not_equal, fill=1.0, base=0,
                               pattern=[[-1, P]], channel_multiplier=1).then_inc(consts, 1)
            sel = select[:, R - 1:R - 1 + TAPS, :]
            pool.affine_select(out=sel, in_=sel, compare_op=ALU.not_equal, fill=1.0, base=0,
                               pattern=[[-1, TAPS], [-TAPS, CG]], channel_multiplier=1).then_inc(consts, 1)

            def block_x(grp, k):
                if k % 2 == 0:
                    pool.wait_ge(x_loaded, LD * (KC * grp + k // 2 + 1))
                pool.wait_ge(x_turned, STEPS * grp + k)
                pool.sem_inc(blocking, 1)
                copy_block(pool, k)

            def wrap_w(n):
                pool.wait_ge(w_loaded[n % NSLOT], LD * (n // NSLOT + 1))
                both = n % GU_LOADS < GU_LOADS - 1 or FC % 2 == 0
                rows = P if both else width(FC - 1)
                v = w_nat[0:rows, n % NSLOT, 0:2 * ROW].rearrange("f (c l) -> f c l", c=2)[:, 0:2 if both else 1, :]
                pool.tensor_copy(v[:, :, L:ROW], v[:, :, 0:PAD]).then_inc(w_wrapped, 1)

            wrap_w(0)
            for k in range(STEPS):
                if k < STEPS - 1:
                    block_x(0, k + 1)
                for u in units_of(k):
                    ahead = u + PERM_AHEAD
                    if ahead < GU_UNITS:
                        if unit_load(ahead) != unit_load(ahead - 1):
                            wrap_w(unit_load(ahead))
                        if permuter(ahead) == "POOL":
                            permute_w(pool, pool.tensor_copy, ahead)
            with pool.Fori(0, G - 1) as g:
                for k in range(STEPS):
                    block_x(g + 1, k)

        @block.tensor
        def _(pe):
            def setup_transposes():
                pe.wait_ge(consts, 7)
                pe.wait_ge(small_in, 4 * LD)
                pe.transpose(xt_ps[0:CG * TAPS, 0:CH], conv_w_nat, ident[0:CH, 0:CH])
                pe.transpose(xt_ps[:, P:P + CH], ctx_w_nat, ident[0:CH, 0:CH])
                pe.transpose(xt_ps[:, 2 * P:3 * P], cond_nat, ident[:]).then_inc(setup_t, 1)

            def setup_products():
                pe.wait_ge(setup_c, 1)
                for q in range(QN):
                    bank, at = (gate_ps, up_ps)[q // (QN // 2)], (q % (QN // 2)) * CH
                    first = QN - 1 - q
                    for n in range(3):
                        mm = pe.matmul(bank[:, at:at + CH], select[:, first:first + R, :], conv_w_t[:, n, :],
                                       start=n == 0, stop=n == 2)
                mm.then_inc(setup_mm, 1)
                for g in range(G):
                    pe.matmul(conv_ps[:, g * P:(g + 1) * P], ctx_w_rep[:, g, :, :], cond_t, start=True, stop=False)
                    mm = pe.matmul(conv_ps[:, g * P:(g + 1) * P], bias_rep[:, g, :, :], ones, start=False, stop=True)
                mm.then_inc(setup_mm, 1)

            def turn_x(grp, k):
                pe.wait_ge(x_blocked, STEPS * grp + k + 1)
                if isinstance(grp, int) and k == 0:
                    pe.wait_ge(setup_c, 1)
                else:
                    pe.wait_ge(xt_lo_done, STEPS * grp + k)
                for b in range(WB):
                    mm = pe.transpose(xt_ps[:, b * P:(b + 1) * P], x_blk[:, b, :, :], ident[:])
                mm.then_inc(x_turned, 1)

            def conv_head(grp):
                pe.wait_ge(t_lo_done, grp + 1)
                pe.wait_ge(xt_lo_done, STEPS * grp + 1)
                if isinstance(grp, int):
                    pe.wait_ge(setup_done, 2)
                else:
                    pe.wait_ge(conv_out, CPG * grp)
                passes = split3(tb_hi, tb_lo, xt_hi, xt_lo)
                for n, (t, v) in enumerate(passes):
                    mm = pe.matmul(conv_ps[:, 0:P], t[:], v[:, 0:P], start=n == 0, stop=n == 2)
                mm.then_inc(conv_done, 1)

            def conv_step(grp, k):
                pe.wait_ge(xt_lo_done, STEPS * grp + min(k + 2, STEPS))
                pe.wait_ge(conv_out, CPG * grp + k + 1)
                at = (k % 2) * WB * P
                for n, (t, v) in enumerate(split3(ta_hi, ta_lo, xt_hi, xt_lo)):
                    pe.matmul(conv_ps[:], t[:], v[:, at:at + WB * P], start=n == 0, stop=False)
                cols = (WB if k < STEPS - 1 else WB - 1) * P
                for n, (t, v) in enumerate(split3(tb_hi, tb_lo, xt_hi, xt_lo)):
                    mm = pe.matmul(conv_ps[:, 0:cols], t[:], v[:, at + P:at + P + cols], start=False, stop=n == 2)
                mm.then_inc(conv_done, 1)

            def turn_w(u):
                n = unit_load(u)
                slot = w_nat[:, n % NSLOT, :]
                if u >= OB:
                    pe.wait_ge(acc_free, u - OB + 1)
                if u < GU_UNITS:
                    pe.wait_ge(w_permuted[permuter(u)], permuted(u))
                    fc = u % FC
                    w = width(fc)
                    for i in range(KC):
                        mm = pe.transpose(acc[:, u % OB, i * P:i * P + w], w_perm[0:w, u % NPERM, i * P:(i + 1) * P],
                                          ident[0:w, 0:w])
                else:
                    pe.wait_ge(w_loaded[n % NSLOT], LD * (n // NSLOT + 1))
                    part = (u - GU_UNITS) % D_PARTS
                    for s, fc in enumerate(range(4 * part, min(4 * part + 4, FC))):
                        w = width(fc)
                        mm = pe.transpose(acc[0:w, u % OB, s * P:(s + 1) * P], slot[:, fc * P:fc * P + w], ident[:])
                mm.then_inc(w_turned, 1)

            def product(bank, which, f, fresh_at=None, last_read=False, mark_first=False):
                w = width(f)
                for i in range(KC):
                    if fresh_at is not None:
                        pe.wait_ge(h_lo_done, fresh_at + i + 1)
                    for n, (wt, hv) in enumerate(split3(wgu_hi, wgu_lo, h_hi, h_lo)):
                        mm = pe.matmul(bank[0:w, :], wt[:, i, which, f * P:f * P + w], hv[:, i, :],
                                       start=i == 0 and n == 0, stop=i == KC - 1 and n == 2)
                        if mark_first and i == 0 and n == 0:
                            mm.then_inc(g_read, 1)
                    if last_read and i < KC - 1:
                        mm.then_inc(h_read, 1)
                return mm

            def down(t, blk, half, f):
                pe.wait_ge(g_lo_done, t + 1)
                w = width(f)
                for tt in range(OB):
                    if f == 0:
                        pe.wait_ge(acc_free, UNITS - OB + OB * blk + tt + 1)
                    at = slice(tt * P, (tt + 1) * P)
                    for n, (gs, wt) in enumerate(((g_hi, wd_hi), (g_hi, wd_lo), (g_lo, wd_hi))):
                        mm = pe.matmul(acc[:, tt, :], gs[0:w, (half * FC + f) % 2, at], wt[0:w, f, :], start=f == 0 and n == 0, stop=f == FC - 1 and n == 2)
                    if f == FC - 1 and tt < OB - 1:
                        mm.then_inc(y_done, 1)
                mm.then_inc(g_read, 1)

            setup_transposes()
            turn_x(0, 0)
            setup_products()
            for k in range(STEPS):
                if k < STEPS - 1:
                    turn_x(0, k + 1)
                for u in units_of(k):
                    turn_w(u)
                if k == 0:
                    conv_head(0)
                conv_step(0, k)
            for u in range(UNITS_PER_STEP * STEPS, UNITS):
                turn_w(u)
            pe.wait_ge(acc_free, UNITS)
            product(gate_ps, 0, 0, fresh_at=0).then_inc(gate_done, 1)
            product(up_ps, 1, 0, mark_first=True).then_inc(up_done, 1)

            def iteration(g, conv):
                for half in range(2):
                    blk = 2 * g + half
                    for f in range(FC):
                        t = blk * FC + f
                        nf = (f + 1) % FC
                        more = conv or half == 0 or f < FC - 1
                        if more:
                            pe.wait_ge(silu_done, t + 1)
                            product(gate_ps, 0, nf, fresh_at=KC * (blk + 1) if nf == 0 else None).then_inc(gate_done, 1)
                        if conv and half == 1 and f < STEPS:
                            turn_x(g + 1, f)
                        if more:
                            pe.wait_ge(g_done, t + 1)
                            product(up_ps, 1, nf, last_read=nf == FC - 1).then_inc(up_done, 1)
                        if conv and half == 1 and f == 0:
                            conv_head(g + 1)
                        if conv and half == 1 and 1 <= f <= STEPS:
                            conv_step(g + 1, f - 1)
                        down(t, blk, half, f)

            with pe.Fori(0, G - 1) as g:
                iteration(g, True)
            iteration(G - 1, False)

        @block.scalar
        def _(act):
            def hi(dst, src):
                return act.activation(dst, src, ACT.Copy)

            def split_toep(grp):
                if isinstance(grp, int):
                    act.wait_ge(setup_done, 1)
                else:
                    act.wait_ge(conv_done, CPG * grp)
                hi(ta_hi[:], toep[:, bass.ds(grp, 1), HALO:QN, :])
                hi(tb_hi[:, TB0:P], toep[:, bass.ds(grp, 1), 0:HALO, :]).then_inc(t_hi_done, 1)

            def split_x(grp, k):
                if k >= 2:
                    act.wait_ge(conv_done, CPG * grp + k)
                elif not isinstance(grp, int):
                    act.wait_ge(conv_done, CPG * grp)
                act.wait_ge(x_turned, STEPS * grp + k + 1)
                at = (k % 2) * WB * P
                last = hi(xt_hi[:, at:at + WB * P], xt_ps[:])
                if k % 2 == 0 and k > 0:
                    last = hi(xt_hi[:, 2 * WB * P:], xt_ps[:, 0:P])
                last.then_inc(xt_hi_done, 1)

            def split_w(u):
                act.wait_ge(w_turned, u + 1)
                for dst, src in weight_views(u, wgu_hi, wd_hi):
                    last = hi(dst, src)
                last.then_inc(w_hi_done, 1)

            def split_h(grp, half, first=False):
                blk = 2 * grp + half
                for i in range(KC):
                    act.wait_ge(staged[i], LD * CG * (grp + 1))
                    if first:
                        act.wait_ge(w_turned, UNITS)
                    elif i < KC - 1:
                        act.wait_ge(h_read, (KC - 1) * (blk - 1) + i + 1)
                    else:
                        act.wait_ge(up_done, FC * blk)
                    hi(h_hi[:, i, :], stage[:, half, i, :]).then_inc(h_hi_done, 1)

            def sigmoid(s, f, first=False):
                act.wait_ge(gate_done, s + 1)
                if not first:
                    act.wait_ge(g_lo_done, s)
                w = width(f)
                act.activation(act_f[0:w, :], gate_ps[0:w, :], ACT.Sigmoid).then_inc(sig_done, 1)

            def split_g(s, f, slot, first=False):
                act.wait_ge(g_done, s + 1)
                if not first:
                    act.wait_ge(g_read, s)
                w = width(f)
                hi(g_hi[0:w, slot, :], act_f[0:w, :]).then_inc(g_hi_done, 1)

            def weights(u):
                ahead = u + PERM_AHEAD
                if ahead < GU_UNITS and permuter(ahead) == "ACT":
                    permute_w(act, hi, ahead)
                split_w(u)
                for n in range(NSLOT, LOADS):
                    if last_unit(n - NSLOT) == u:
                        load_w(act, n)

            act.wait_ge(consts, 7)
            act.activation(head[0:1, 0:1], ones[0:1, 0:1], ACT.Sigmoid)
            split_x(0, 0)
            for u in range(PERM_AHEAD):
                if permuter(u) == "ACT":
                    permute_w(act, hi, u)
            split_toep(0)
            for k in range(STEPS):
                if k < STEPS - 1:
                    split_x(0, k + 1)
                if k % 2 == 0 and k < STEPS - 2:
                    act.wait_ge(x_blocked, k + 2)
                    load_x(act, 0, k // 2 + 1)
                for u in units_of(k):
                    weights(u)
            for u in range(UNITS_PER_STEP * STEPS, UNITS):
                weights(u)
            split_h(0, 0, first=True)
            sigmoid(0, 0, first=True)
            split_g(0, 0, 0, first=True)

            def iteration(g, conv):
                for half in range(2):
                    for f in range(FC):
                        s, nf = (2 * g + half) * FC + f + 1, (f + 1) % FC
                        if conv or half == 0 or f < FC - 1:
                            sigmoid(s, nf)
                            if conv and half == 0 and f == 0:
                                split_toep(g + 1)
                            if conv and half == 1 and f < STEPS:
                                split_x(g + 1, f)
                            if nf == FC - 1 and half == 0:
                                split_h(g, 1)
                            if nf == FC - 1 and half == 1 and conv:
                                split_h(g + 1, 0)
                            split_g(s, nf, (half * FC + f + 1) % 2)

            with act.Fori(0, G - 1) as g:
                iteration(g, True)
            iteration(G - 1, False)

        @block.vector
        def _(dve):
            def lo(dst, src, hi_part):
                return dve.tensor_tensor(dst, src, hi_part.bitcast(F32), ALU.subtract)

            def turn_small():
                dve.wait_ge(setup_t, 1)
                for n in range(3):
                    rest = xt_ps[0:CG * TAPS, 0:CH] if n == 0 else conv_w_rest[:, n - 1, :]
                    dve.tensor_copy(conv_w_t[:, n, :], rest).then_inc(parts, 1)
                    if n < 2:
                        dve.wait_ge(parts, 2 * n + 1)
                        dve.tensor_tensor(conv_w_rest[:, n, :], rest, conv_w_t[:, n, :], ALU.subtract).then_inc(parts, 1)
                        dve.wait_ge(parts, 2 * n + 2)
                dve.tensor_copy(cond_t, xt_ps[:, 2 * P:3 * P])
                dve.tensor_copy(ctx_w_rep, xt_ps[:, P:P + CH].rearrange("d (g a o) -> d g a o", g=G, a=1)
                                .broadcast_to([P, G, R, CG]))
                dve.wait_ge(small_in, 4 * LD)
                dve.tensor_copy(bias_rep, bias_nat.rearrange("d (g a o) -> d g a o", g=G, a=1)
                                .broadcast_to([1, G, R, CG])).then_inc(setup_c, 1)

            def finish_setup():
                dve.wait_ge(setup_mm, 1)
                for n, bank in enumerate((gate_ps, up_ps)):
                    q0 = n * (QN // 2)
                    last = dve.tensor_copy(toep[:, :, q0:q0 + QN // 2, :],
                                           bank[:, 0:QN // 2 * CH].rearrange("p (q g o) -> p g q o", g=G, o=CG))
                last.then_inc(setup_done, 1)
                dve.wait_ge(setup_mm, 2)
                dve.tensor_copy(ctxb[:].rearrange("p g n -> p (g n)"), conv_ps[:]).then_inc(setup_done, 1)

            def split_toep(grp):
                if isinstance(grp, int):
                    dve.wait_ge(setup_done, 2)
                dve.wait_ge(t_hi_done, grp + 1)
                lo(ta_lo[:].rearrange("p (q o) -> p q o", o=CG), toep[:, bass.ds(grp, 1), HALO:QN, :],
                   ta_hi[:].rearrange("p (q o) -> p q o", o=CG))
                lo(tb_lo[:, TB0:P], toep[:, bass.ds(grp, 1), 0:HALO, :], tb_hi[:, TB0:P]).then_inc(t_lo_done, 1)

            def split_x(grp, k):
                dve.wait_ge(xt_hi_done, STEPS * grp + k + 1)
                at = (k % 2) * WB * P
                last = lo(xt_lo[:, at:at + WB * P], xt_ps[:], xt_hi[:, at:at + WB * P])
                if k % 2 == 0 and k > 0:
                    last = lo(xt_lo[:, 2 * WB * P:], xt_ps[:, 0:P], xt_hi[:, 2 * WB * P:])
                last.then_inc(xt_lo_done, 1)

            def split_w(u):
                dve.wait_ge(w_hi_done, u + 1)
                for (dst, src), (hi_part, _) in zip(weight_views(u, wgu_lo, wd_lo), weight_views(u, wgu_hi, wd_hi)):
                    last = lo(dst, src, hi_part)
                last.then_inc(acc_free, 1)

            def read_head(grp):
                dve.wait_ge(conv_done, CPG * grp + 1)
                dve.tensor_tensor(head[HEAD0:P, :], conv_ps[HEAD0:P, 0:P], ctxb[HEAD0:P, bass.ds(grp, 1), :],
                                  ALU.add).then_inc(conv_out, 1)

            def read_conv(grp, k):
                i = k // 2
                if k % 2 == 0 and isinstance(grp, int):
                    if i == KC - 1:
                        dve.wait_ge(staged[0], LD * CG)
                elif k % 2 == 0 and i > 0:
                    dve.wait_ge(staged[i - 1], LD * CG * (grp + 1))
                elif k % 2 == 0:
                    dve.wait_ge(staged[KC - 1], LD * CG * grp)
                dve.wait_ge(conv_done, CPG * grp + k + 2)
                to = windows(grp, i)
                w0, n = (k % 2) * WB, WB if k < STEPS - 1 else WB - 1
                last = dve.tensor_tensor(to[:, w0:w0 + n, :], conv_ps[:, 0:n * P].rearrange("p (w n) -> p w n", w=n),
                                         ctxb[:, bass.ds(grp, 1), :].broadcast_to([P, n, P]), ALU.add)
                if k == STEPS - 1:
                    dve.tensor_tensor(to[0:HEAD0, JJ - 1, :], conv_ps[0:HEAD0, n * P:(n + 1) * P],
                                      ctxb[0:HEAD0, bass.ds(grp, 1), :], ALU.add)
                    dve.wait_ge(conv_out, CPG * grp + 1)
                    last = dve.tensor_copy(to[HEAD0:P, JJ - 1, :], head[HEAD0:P, :])
                last.then_inc(conv_out, 1)

            def split_h(blk, half):
                for i in range(KC):
                    dve.wait_ge(h_hi_done, KC * blk + i + 1)
                    lo(h_lo[:, i, :], stage[:, half, i, :], h_hi[:, i, :]).then_inc(h_lo_done, 1)

            def silu(s, f):
                dve.wait_ge(sig_done, s + 1)
                w = width(f)
                dve.tensor_tensor(act_f[0:w, :], gate_ps[0:w, :], act_f[0:w, :], ALU.mult).then_inc(silu_done, 1)

            def gated(s, f):
                dve.wait_ge(up_done, s + 1)
                dve.wait_ge(silu_done, s + 1)
                w = width(f)
                dve.tensor_tensor(act_f[0:w, :], up_ps[0:w, :], act_f[0:w, :], ALU.mult).then_inc(g_done, 1)

            def split_g(s, f, slot):
                dve.wait_ge(g_hi_done, s + 1)
                w = width(f)
                lo(g_lo[0:w, slot, :], act_f[0:w, :], g_hi[0:w, slot, :]).then_inc(g_lo_done, 1)

            def add_residual(blk):
                for tt in range(OB):
                    dve.wait_ge(res_loaded[tt], LD * (blk + 1))
                    if tt < OB - 1:
                        dve.wait_ge(y_done, (OB - 1) * blk + tt + 1)
                    else:
                        dve.wait_ge(g_read, FC * (blk + 1) + 1)
                    dve.tensor_tensor(res[:, tt, :], acc[:, tt, :], res[:, tt, :], ALU.add).then_inc(acc_free, 1)

            dve.wait_ge(x_loaded, LD)
            copy_block(dve, 0)
            turn_small()
            split_x(0, 0)
            finish_setup()
            split_toep(0)
            for k in range(STEPS):
                if k < STEPS - 1:
                    split_x(0, k + 1)
                for u in units_of(k):
                    split_w(u)
                if k == 0:
                    read_head(0)
                read_conv(0, k)
            for u in range(UNITS_PER_STEP * STEPS, UNITS):
                split_w(u)
            split_h(0, 0)
            silu(0, 0)
            gated(0, 0)
            split_g(0, 0, 0)

            def iteration(g, conv):
                for half in range(2):
                    blk = 2 * g + half
                    for f in range(FC):
                        s, nf = blk * FC + f + 1, (f + 1) % FC
                        if conv or half == 0 or f < FC - 1:
                            silu(s, nf)
                            if conv and half == 0 and f == 0:
                                split_toep(g + 1)
                            if conv and half == 1 and f < STEPS:
                                split_x(g + 1, f)
                            if nf == FC - 1 and (half == 0 or conv):
                                split_h(blk + 1, 1 - half)
                            gated(s, nf)
                            if conv and half == 1 and f == 0:
                                read_head(g + 1)
                            if conv and half == 1 and 1 <= f <= STEPS:
                                read_conv(g + 1, f - 1)
                            split_g(s, nf, (half * FC + f + 1) % 2)
                    add_residual(blk)

            with dve.Fori(0, G - 1) as g:
                iteration(g, True)
            iteration(G - 1, False)


_INS = ["x", "cond_128", "fside_S_0", "L0_cond_weight", "L0_cond_c_weight", "L0_ffn_W_gate", "L0_ffn_W_up", "L0_ffn_W_down"]


def kernel(**inputs):
    import numpy as np
    import concourse.bacc as bacc
    from concourse.bass_utils import run_bass_kernel_spmd

    nc = bacc.Bacc("TRN2", target_bir_lowering=False, num_devices=1)
    arrays, args = {}, []
    for name in _INS:
        a = np.ascontiguousarray(inputs[name])
        arrays[f"in_{name}"] = a
        args.append(nc.dram_tensor(f"in_{name}", a.shape, mybir.dt.from_np(a.dtype), kind="ExternalInput").ap())
    args.append(nc.dram_tensor("out_y", inputs["x"].shape, F32, kind="ExternalOutput").ap())
    adaln_ffn(nc, *args)
    r = run_bass_kernel_spmd(nc, [arrays], core_ids=[0])
    return r.results[0]["out_y"]
```

```python
from contextlib import ExitStack

import concourse.bass as bass
from concourse import mybir

F32 = mybir.dt.float32
F32R = mybir.dt.float32r
BF16 = mybir.dt.bfloat16
ALU = mybir.AluOpType
ACT = mybir.ActivationFunctionType

P = 128


def adaln_ffn(nc, x, cond, bias, conv_w, ctx_w, w_gate, w_up, w_down, out):
    N, CH, L = x.shape
    _, CG, TAPS = conv_w.shape
    F = w_gate.shape[0]
    G = CH // CG
    PAD = TAPS // 2
    R = P // CG
    KC = L // P
    JJ = P // R
    WB = 4
    STEPS = L // R // WB
    TOK = WB * P
    OB = TOK // N
    FC = -(-F // P)
    HEAD_P = R - PAD
    HEAD0 = HEAD_P * CG
    HALO = TAPS - 1
    QN = HALO + R
    TB0 = (R - HALO) * CG
    ROW = L + PAD
    assert N == P and CG == 8 and R == 16 and KC == 4 and QN % 2 == 0 and G * CG == conv_w.shape[0]

    def width(fc):
        return min(P, F - fc * P)

    GATE, UP, DOWN = range(3)
    EC = 6
    E = 2 * EC
    PER_STEP = (2, 1, 1, 1, 1, 1, 1, 1)
    NPERM = 3
    PERM_AHEAD = 2
    NLATE = 4
    NDOWN = 2
    assert EC >= 3

    def late_before_up(f):
        return [(GATE, f + 2)] if EC <= f + 2 < FC else []

    def late_after_up(f):
        return ([(UP, f + 2)] if EC <= f + 2 < FC else []) + ([(DOWN, f + 1)] if 1 < f + 1 < FC else [])

    units = [(kind, fc) for fc in range(EC) for kind in (GATE, UP)] + [(DOWN, 0), (DOWN, 1)]
    for f in range(FC):
        units += late_before_up(f) + late_after_up(f)
    UNITS = len(units)
    number = {unit: n for n, unit in enumerate(units)}

    def gu(v):
        return (v % 2, v // 2)

    def permuter(v):
        return "POOL" if v >= E and v % 2 == 1 else "ACT"

    def permuted(v):
        return sum(permuter(w) == permuter(v) for w in range(v + 1))

    def early_at(k):
        first = sum(PER_STEP[:k])
        return range(min(first, E), min(first + PER_STEP[k], E) if k < STEPS else E)

    def early_h(k):
        return {STEPS - 3: [0], STEPS - 1: [1]}.get(k, [])

    with ExitStack() as ctx:
        def sb(name, shape, dt=F32, stack=ctx):
            return stack.enter_context(nc.sbuf_tensor(name, shape, dt))

        def ps(name, shape):
            return ctx.enter_context(nc.psum_tensor(name, shape, F32))

        def sem(name):
            return ctx.enter_context(nc.semaphore(name))

        wgu_hi = sb("wgu_hi", [P, KC, 2, F], F32R)
        wgu_lo = sb("wgu_lo", [P, KC, 2, F], F32R)
        with ExitStack() as early:
            w_early = sb("w_early", [P, E, ROW], F32, early)
            perm_early = sb("perm_early", [P, NPERM, L], F32, early)
            x_first = sb("x_first", [P, KC - 1, CG, P], F32, early)
        wd_hi = sb("wd_hi", [P, FC, L], F32R)
        wd_lo = sb("wd_lo", [P, FC, L], F32R)
        h_hi = sb("h_hi", [P, KC, TOK], F32R)
        h_lo = sb("h_lo", [P, KC, TOK], F32R)
        g_hi = sb("g_hi", [P, 2, TOK], F32R)
        g_lo = sb("g_lo", [P, 2, TOK], F32R)
        stage = sb("stage", [P, 2, KC, TOK])
        with ExitStack() as late:
            down_nat = sb("down_nat", [P, NDOWN, KC, P], F32, late)
            w_late = sb("w_late", [P, NLATE, ROW], F32, late)
            perm_late = sb("perm_late", [P, NPERM, L], F32, late)
        xt_hi = sb("xt_hi", [P, (2 * WB + 1) * P], F32R)
        xt_lo = sb("xt_lo", [P, (2 * WB + 1) * P], F32R)
        x_in = sb("x_in", [P, CG, P])
        x_blk = sb("x_blk", [P, WB, R, CG])
        win = sb("win", [P, JJ, P])
        head = sb("head", [P, P])
        act_f = sb("act_f", [P, TOK])
        res = sb("res", [P, OB, L])
        ctxb = sb("ctxb", [P, G, P])
        bias_col = sb("bias_col", [P, G, 1])
        toep = sb("toep", [P, G, QN, CG])
        ta_hi = sb("ta_hi", [P, P], F32R)
        ta_lo = sb("ta_lo", [P, P], F32R)
        tb_hi = sb("tb_hi", [P, P], F32R)
        tb_lo = sb("tb_lo", [P, P], F32R)
        ident = sb("ident", [P, P])

        ctx_w_rep = res[:, 0, :].rearrange("d (g p o) -> d g p o", g=G, p=R)
        cond_nat = res[:, 1, 0:P]
        cond_t = res[:, 1, P:2 * P]
        ctx_w_nat = res[0:CH, 1, 256:384]
        conv_w_t = res[0:CG * TAPS, 1, 384:384 + 3 * CH // 2].bitcast(BF16).rearrange("k (a o) -> k a o", a=3)
        conv_w_nat = res[0:CH, 1, 432:432 + CG * TAPS]
        conv_w_rest = res[0:CG * TAPS, 2, 160:160 + 2 * CH].rearrange("k (a o) -> k a o", a=2)
        SEL_W = QN + R - 1
        select = res[0:CG * TAPS, 2, 0:CG * SEL_W // 2].bitcast(BF16).rearrange("k (s c) -> k s c", c=CG)

        acc = ps("acc", [P, OB, L])
        gate_ps = ps("gate_ps", [P, TOK])
        up_ps = ps("up_ps", [P, TOK])
        xt_ps = ps("xt_ps", [P, WB * P])
        conv_ps = ps("conv_ps", [P, WB * P])

        small_in = sem("small_in")
        consts = sem("consts")
        setup_t = sem("setup_t")
        parts = sem("parts")
        ctx_w_ready = sem("ctx_w_ready")
        cond_ready = sem("cond_ready")
        conv_w_ready = sem("conv_w_ready")
        ctx_mm = sem("ctx_mm")
        toep_mm = sem("toep_mm")
        bias_loaded = sem("bias_loaded")
        ctx_done = sem("ctx_done")
        toep_done = sem("toep_done")
        w_loaded = [sem(f"w_loaded{i}") for i in range(E)]
        late_loaded = [sem(f"late_loaded{i}") for i in range(NLATE)]
        down_loaded = [sem(f"down_loaded{i}") for i in range(NDOWN)]
        w_wrapped = sem("w_wrapped")
        w_permuted = {e: sem(f"w_permuted_{e}") for e in ("ACT", "POOL")}
        w_turned = sem("w_turned")
        w_hi_done = sem("w_hi_done")
        w_lo_done = sem("w_lo_done")
        acc_free = sem("acc_free")
        x_first_loaded = [sem(f"x_first_loaded{i}") for i in range(KC)]
        x_loaded = sem("x_loaded")
        blocking = sem("blocking")
        x_blocked = sem("x_blocked")
        x_turned = sem("x_turned")
        xt_hi_done = sem("xt_hi_done")
        xt_lo_done = sem("xt_lo_done")
        t_hi_done = sem("t_hi_done")
        t_lo_done = sem("t_lo_done")
        conv_done = sem("conv_done")
        conv_out = sem("conv_out")
        staged = [[sem(f"staged{half}_{i}") for i in range(KC)] for half in range(2)]
        h_hi_done = sem("h_hi_done")
        h_lo_done = sem("h_lo_done")
        h_read = sem("h_read")
        gate_done = sem("gate_done")
        sig_done = sem("sig_done")
        silu_done = sem("silu_done")
        up_done = sem("up_done")
        g_done = sem("g_done")
        g_hi_done = sem("g_hi_done")
        g_lo_done = sem("g_lo_done")
        g_read = sem("g_read")
        y_done = sem("y_done")
        res_loaded = [sem(f"res_loaded{i}") for i in range(OB)]
        y_stored = [sem(f"y_stored{i}") for i in range(OB)]

        def weight_views(u, wgu, wd):
            kind, fc = units[u]
            w = width(fc)
            if u < E:
                bank = acc[:, u % OB, :]
            else:
                bank = (xt_ps, conv_ps)[(u - E) % 2][:]
            if kind == DOWN:
                return wd[0:w, fc, :], bank[0:w, :]
            return wgu[:, :, kind, fc * P:fc * P + w], bank.rearrange("p (i f) -> p i f", f=P)[:, :, 0:w]

        CPG = STEPS + 1
        LD = 16

        def split3(hi_w, lo_w, hi_x, lo_x):
            return ((hi_w, hi_x), (lo_w, hi_x), (hi_w, lo_x))

        def x_place(grp, i):
            return x_first[:, i - 1] if isinstance(grp, int) and i > 0 else x_in[:]

        def load_x(eng, grp, i):
            eng.dma_start(x_place(grp, i), x[:, bass.ds(grp * CG, CG), i * P:(i + 1) * P]
                          ).then_inc(x_first_loaded[i] if isinstance(grp, int) else x_loaded, LD)

        def blocks(grp, k):
            if isinstance(grp, int) and k % 2 == 1:
                return act_f[:].rearrange("n (b r c) -> n b r c", b=WB, r=R)
            return x_blk

        def copy_block(copy, grp, k):
            r0 = (k % 2) * WB * R
            copy(blocks(grp, k)[:, :, :, :], x_place(grp, k // 2)[:, :, r0:r0 + WB * R]
                 .rearrange("n c (b r) -> n b r c", r=R)).then_inc(x_blocked, 1)

        def w_nat(v):
            return w_early[:, v, :] if v < E else w_late[:, (v - E) % NLATE, :]

        def w_perm(v):
            return perm_early[:, v % NPERM, :] if v < E else perm_late[:, (v - E) % NPERM, :]

        def permute_w(eng, copy, v):
            w = width(v // 2)
            eng.wait_ge(w_wrapped, v + 1)
            if v >= E + NPERM or NPERM <= v < E:
                eng.wait_ge(w_turned, number[gu(v - NPERM)] + 1)
            copy(w_perm(v)[0:w].rearrange("f (i p j) -> f i p j", i=KC, p=R),
                 w_nat(v)[0:w, PAD:ROW].rearrange("f (i j p) -> f i p j", i=KC, p=R)
                 ).then_inc(w_permuted[permuter(v)], 1)

        def load_w(eng, v):
            kind, fc = gu(v)
            w = width(fc)
            if v >= E + NLATE:
                eng.wait_ge(w_turned, number[gu(v - NLATE)] + 1)
            done = w_loaded[v] if v < E else late_loaded[(v - E) % NLATE]
            eng.dma_start(w_nat(v)[0:w, 0:L], (w_gate, w_up)[kind][fc * P:fc * P + w, :]).then_inc(done, LD)

        def conv_bank(grp, k):
            return gate_ps if isinstance(grp, int) and k % 2 == 0 else conv_ps

        def windows(grp, i):
            if isinstance(grp, int) and i in (1, 2):
                return res[:, 2 * i - 2:2 * i, :].rearrange("p a (w n) -> p (a w) n", n=P)
            if isinstance(grp, int) and i == 0:
                return x_in
            return win

        block = ctx.enter_context(nc.Block())

        @block.sync
        def _(sp):
            def stage_chunk(grp, i, channels=range(CG)):
                sp.wait_ge(conv_out, CPG * grp + 2 * i + 3)
                for o in channels:
                    sp.dma_start(stage[:, o // OB, i, (o % OB) * P:(o % OB + 1) * P],
                                 windows(grp, i)[o:P:CG, :, :]).then_inc(staged[o // OB][i], LD)

            def load_res(blk):
                for tt in range(OB):
                    sp.dma_start(res[:, tt, :], x[:, bass.ds(blk * OB + tt, 1), :]).then_inc(res_loaded[tt], LD)

            def store_y(blk, last=False):
                for tt in range(OB):
                    sp.wait_ge(acc_free, OB * blk + tt + 1)
                    sp.dma_start(out[:, bass.ds(blk * OB + tt, 1), :], res[:, tt, :]).then_inc(y_stored[tt], LD)
                for tt in range(OB):
                    sp.wait_ge(y_stored[tt], LD * (blk + 1))
                if not last:
                    load_res(blk + 1)

            def load_down(fc):
                w = width(fc)
                if fc < NDOWN:
                    sp.wait_ge(conv_done, CPG)
                else:
                    sp.wait_ge(w_turned, number[DOWN, fc - NDOWN] + 1)
                sp.dma_start(down_nat[:, fc % NDOWN, :, 0:w], w_down[:, fc * P:fc * P + w].rearrange("(q d) f -> d q f", d=P)
                             ).then_inc(down_loaded[fc % NDOWN], LD)

            sp.dma_start(conv_w_nat, conv_w.rearrange("o c k -> o (c k)")).then_inc(small_in, LD)
            sp.dma_start(ctx_w_nat, ctx_w).then_inc(small_in, LD)
            sp.dma_start(cond_nat, cond).then_inc(small_in, LD)
            load_x(sp, 0, 0)
            for i in range(1, KC):
                load_w(sp, 2 * i - 2)
                load_w(sp, 2 * i - 1)
                load_x(sp, 0, i)
                if i == 1:
                    for g in range(G):
                        sp.dma_start(bias_col[:, g, :], bias[g * CG:(g + 1) * CG].rearrange("(a o b) -> a o b", a=1, b=1)
                                     .broadcast_to([R, CG, 1])).then_inc(bias_loaded, LD)
            for v in range(2 * KC - 2, E):
                load_w(sp, v)
            for i in range(KC):
                stage_chunk(0, i, range(OB))
            for fc in range(NDOWN):
                load_down(fc)
            for i in range(KC):
                stage_chunk(0, i, range(OB, CG))
            for half in range(2):
                for i in range(KC):
                    sp.wait_ge(staged[half][i], LD * OB)
            load_res(0)
            for kind, fc in units[E:]:
                if kind == DOWN and fc >= NDOWN:
                    load_down(fc)
                elif kind != DOWN:
                    load_w(sp, 2 * fc + kind)
            sp.wait_ge(w_turned, UNITS)

            def iteration(g, conv):
                if conv:
                    sp.wait_ge(x_blocked, STEPS * (g + 1))
                    load_x(sp, g + 1, 0)
                store_y(2 * g)
                if conv:
                    for i in range(KC):
                        if i < KC - 1:
                            sp.wait_ge(x_blocked, STEPS * (g + 1) + 2 * i + 2)
                            load_x(sp, g + 1, i + 1)
                        if i == 0:
                            sp.wait_ge(h_lo_done, 2 * KC * (g + 1))
                        stage_chunk(g + 1, i)
                store_y(2 * g + 1, last=not conv)

            with sp.Fori(0, G - 1) as g:
                iteration(g, True)
            iteration(G - 1, False)

        @block.gpsimd
        def _(pool):
            pool.memset(ident[:], 0.0).then_inc(consts, 1)
            pool.memset(res[0:CG * TAPS, 2, 0:CG * SEL_W // 2], 0.0).then_inc(consts, 1)
            pool.memset(tb_hi[:, 0:TB0].bitcast(F32), 0.0).then_inc(consts, 1)
            pool.memset(tb_lo[:, 0:TB0].bitcast(F32), 0.0).then_inc(consts, 1)
            pool.wait_ge(consts, 4)
            pool.affine_select(out=ident[:], in_=ident[:], compare_op=ALU.not_equal, fill=1.0, base=0,
                               pattern=[[-1, P]], channel_multiplier=1).then_inc(consts, 1)
            sel = select[:, R - 1:R - 1 + TAPS, :]
            pool.affine_select(out=sel, in_=sel, compare_op=ALU.not_equal, fill=1.0, base=0,
                               pattern=[[-1, TAPS], [-TAPS, CG]], channel_multiplier=1).then_inc(consts, 1)

            def block_x(grp, k):
                if isinstance(grp, int):
                    pool.wait_ge(x_first_loaded[k // 2], LD)
                elif k % 2 == 0:
                    pool.wait_ge(x_loaded, LD * (KC * (grp - 1) + k // 2 + 1))
                if not isinstance(grp, int):
                    pool.wait_ge(x_turned, STEPS * grp + k)
                elif k == 1:
                    pool.wait_ge(x_blocked, 1)
                else:
                    pool.wait_ge(x_turned, k - 1)
                pool.sem_inc(blocking, 1)
                copy_block(pool.tensor_copy, grp, k)

            def wrap_w(v):
                if v < E:
                    pool.wait_ge(w_loaded[v], LD)
                else:
                    pool.wait_ge(late_loaded[(v - E) % NLATE], LD * ((v - E) // NLATE + 1))
                w = width(v // 2)
                pool.tensor_copy(w_nat(v)[0:w, L:ROW], w_nat(v)[0:w, 0:PAD]).then_inc(w_wrapped, 1)

            for v in range(PERM_AHEAD):
                wrap_w(v)
            for k in range(STEPS + 1):
                if k < STEPS - 1:
                    block_x(0, k + 1)
                for u in early_at(k):
                    if u + PERM_AHEAD < E:
                        wrap_w(u + PERM_AHEAD)
            for v in range(E, 2 * FC):
                wrap_w(v)
                if permuter(v) == "POOL":
                    permute_w(pool, pool.tensor_copy, v)
            with pool.Fori(0, G - 1) as g:
                for k in range(STEPS):
                    block_x(g + 1, k)

        @block.tensor
        def _(pe):
            def setup_transposes():
                pe.wait_ge(consts, 6)
                pe.wait_ge(small_in, 3 * LD)
                pe.transpose(xt_ps[0:CG * TAPS, 0:CH], conv_w_nat, ident[0:CH, 0:CH])
                pe.transpose(xt_ps[:, P:P + CH], ctx_w_nat, ident[0:CH, 0:CH])
                pe.transpose(gate_ps[:, 0:P], cond_nat, ident[:]).then_inc(setup_t, 1)

            def ctx_products():
                pe.wait_ge(ctx_w_ready, 1)
                pe.wait_ge(cond_ready, 1)
                for g in range(G):
                    mm = pe.matmul(conv_ps[:, g * P:(g + 1) * P], ctx_w_rep[:, g, :, :], cond_t, start=True, stop=True)
                mm.then_inc(ctx_mm, 1)

            def toep_products():
                pe.wait_ge(conv_w_ready, 1)
                for q in range(QN):
                    bank, at = (gate_ps, up_ps)[q // (QN // 2)], (q % (QN // 2)) * CH
                    first = QN - 1 - q
                    for n in range(3):
                        mm = pe.matmul(bank[:, at:at + CH], select[:, first:first + R, :], conv_w_t[:, n, :],
                                       start=n == 0, stop=n == 2)
                mm.then_inc(toep_mm, 1)

            def turn_x(grp, k):
                pe.wait_ge(x_blocked, STEPS * grp + k + 1)
                if isinstance(grp, int) and k == 0:
                    pe.wait_ge(conv_w_ready, 1)
                    pe.wait_ge(cond_ready, 1)
                else:
                    pe.wait_ge(xt_lo_done, STEPS * grp + k)
                for b in range(WB):
                    mm = pe.transpose(xt_ps[:, b * P:(b + 1) * P], blocks(grp, k)[:, b, :, :], ident[:])
                mm.then_inc(x_turned, 1)

            def conv_head(grp):
                pe.wait_ge(t_lo_done, grp + 1)
                pe.wait_ge(xt_lo_done, STEPS * grp + 1)
                if isinstance(grp, int):
                    pe.wait_ge(ctx_done, 1)
                else:
                    pe.wait_ge(conv_out, CPG * grp)
                passes = split3(tb_hi, tb_lo, xt_hi, xt_lo)
                for n, (t, v) in enumerate(passes):
                    mm = pe.matmul(conv_ps[:, 0:P], t[:], v[:, 0:P], start=n == 0, stop=n == 2)
                mm.then_inc(conv_done, 1)

            def conv_step(grp, k):
                bank = conv_bank(grp, k)
                if not isinstance(grp, int):
                    pe.wait_ge(conv_out, CPG * grp + k + 1)
                elif k > 0:
                    pe.wait_ge(conv_out, k)
                at = (k % 2) * WB * P
                for n, (t, v) in enumerate(split3(ta_hi, ta_lo, xt_hi, xt_lo)):
                    pe.matmul(bank[:], t[:], v[:, at:at + WB * P], start=n == 0, stop=False)
                cols = (WB if k < STEPS - 1 else WB - 1) * P
                for n, (t, v) in enumerate(split3(tb_hi, tb_lo, xt_hi, xt_lo)):
                    if n == 0:
                        pe.wait_ge(xt_hi_done, STEPS * grp + min(k + 2, STEPS))
                    elif n == 2:
                        pe.wait_ge(xt_lo_done, STEPS * grp + min(k + 2, STEPS))
                    mm = pe.matmul(bank[:, 0:cols], t[:], v[:, at + P:at + P + cols], start=False, stop=n == 2)
                mm.then_inc(conv_done, 1)

            def turn_w(u):
                kind, fc = units[u]
                w = width(fc)
                _, bank = weight_views(u, wgu_hi, wd_hi)
                if u >= E + 2:
                    pe.wait_ge(w_lo_done, u - 1)
                elif u == E:
                    pe.wait_ge(xt_lo_done, STEPS)
                elif u == E + 1:
                    pe.wait_ge(conv_out, CPG)
                elif u >= OB:
                    pe.wait_ge(w_lo_done, u - OB + 1)
                if kind == DOWN:
                    pe.wait_ge(down_loaded[fc % NDOWN], LD * (fc // NDOWN + 1))
                    for dq in range(KC):
                        mm = pe.transpose(bank[:, dq * P:(dq + 1) * P], down_nat[:, fc % NDOWN, dq, 0:w], ident[:])
                else:
                    v = 2 * fc + kind
                    pe.wait_ge(w_permuted[permuter(v)], permuted(v))
                    for i in range(KC):
                        mm = pe.transpose(bank[:, i, :], w_perm(v)[0:w, i * P:(i + 1) * P], ident[0:w, 0:w])
                mm.then_inc(w_turned, 1)

            def product(bank, which, f, chunks=range(KC), fresh_at=None, last_read=False, new_w=False):
                w = width(f)
                if new_w:
                    pe.wait_ge(w_lo_done, number[which, f] + 1)
                for i in chunks:
                    if fresh_at is not None:
                        pe.wait_ge(h_lo_done, fresh_at + i + 1)
                    for n, (wt, hv) in enumerate(split3(wgu_hi, wgu_lo, h_hi, h_lo)):
                        mm = pe.matmul(bank[0:w, :], wt[:, i, which, f * P:f * P + w], hv[:, i, :],
                                       start=i == 0 and n == 0, stop=i == KC - 1 and n == 2)
                    if last_read and i < KC - 1:
                        mm.then_inc(h_read, 1)
                return mm

            def down(t, blk, half, f, new_w=False):
                pe.wait_ge(g_lo_done, t + 1)
                if new_w:
                    pe.wait_ge(w_lo_done, number[DOWN, f] + 1)
                w = width(f)
                for tt in range(OB):
                    if f == 0 and not new_w:
                        pe.wait_ge(acc_free, OB * blk - OB + tt + 1)
                    at = slice(tt * P, (tt + 1) * P)
                    for n, (gs, wt) in enumerate(((g_hi, wd_hi), (g_hi, wd_lo), (g_lo, wd_hi))):
                        mm = pe.matmul(acc[:, tt, :], gs[0:w, (half * FC + f) % 2, at], wt[0:w, f, :],
                                       start=f == 0 and n == 0, stop=f == FC - 1 and n == 2)
                    if f == FC - 1 and tt < OB - 1:
                        mm.then_inc(y_done, 1)
                mm.then_inc(g_read, 1)

            setup_transposes()
            ctx_products()
            turn_x(0, 0)
            toep_products()
            for k in range(STEPS):
                if k < STEPS - 1:
                    turn_x(0, k + 1)
                for u in early_at(k):
                    turn_w(u)
                if k == 0:
                    conv_head(0)
                conv_step(0, k)
            for u in early_at(STEPS):
                turn_w(u)
            pe.wait_ge(conv_out, STEPS)
            for chunks in (range(KC - 2), [KC - 2]):
                product(gate_ps, GATE, 0, chunks, fresh_at=0, new_w=True)
                product(up_ps, UP, 0, chunks, new_w=True)
            turn_w(number[DOWN, 0])
            product(gate_ps, GATE, 0, [KC - 1], fresh_at=0).then_inc(gate_done, 1)
            product(up_ps, UP, 0, [KC - 1]).then_inc(up_done, 1)
            turn_w(number[DOWN, 1])

            def ffn_block(g, half, conv, new_w=False):
                blk = 2 * g + half
                for f in range(FC):
                    t = blk * FC + f
                    nf = (f + 1) % FC
                    more = conv or half == 0 or f < FC - 1
                    if more:
                        pe.wait_ge(silu_done, t + 1)
                        product(gate_ps, GATE, nf, fresh_at=KC * (blk + 1) if nf == 0 else None,
                                new_w=new_w and nf > 0).then_inc(gate_done, 1)
                    if new_w:
                        for unit in late_before_up(f):
                            turn_w(number[unit])
                    if conv and half == 1 and f == 0:
                        pe.wait_ge(w_lo_done, UNITS)
                    if conv and half == 1 and f < STEPS:
                        turn_x(g + 1, f)
                    if more:
                        pe.wait_ge(g_done, t + 1)
                        product(up_ps, UP, nf, last_read=nf == FC - 1, new_w=new_w and nf > 0).then_inc(up_done, 1)
                    if new_w:
                        for unit in late_after_up(f):
                            turn_w(number[unit])
                    if conv and half == 1 and f == 0:
                        conv_head(g + 1)
                    if conv and half == 1 and 1 <= f <= STEPS:
                        conv_step(g + 1, f - 1)
                    down(t, blk, half, f, new_w=new_w)

            ffn_block(0, 0, True, new_w=True)
            with pe.Fori(0, G - 1) as g:
                ffn_block(g, 1, True)
                ffn_block(g + 1, 0, True)
            ffn_block(G - 1, 1, False)

        @block.scalar
        def _(act):
            def hi(dst, src):
                return act.activation(dst, src, ACT.Copy)

            def split_toep(grp):
                if isinstance(grp, int):
                    act.wait_ge(toep_done, 1)
                else:
                    act.wait_ge(conv_done, CPG * grp)
                hi(ta_hi[:], toep[:, bass.ds(grp, 1), HALO:QN, :])
                hi(tb_hi[:, TB0:P], toep[:, bass.ds(grp, 1), 0:HALO, :]).then_inc(t_hi_done, 1)

            def split_x(grp, k):
                if k >= 2:
                    act.wait_ge(conv_done, CPG * grp + k)
                elif not isinstance(grp, int):
                    act.wait_ge(conv_done, CPG * grp)
                act.wait_ge(x_turned, STEPS * grp + k + 1)
                at = (k % 2) * WB * P
                last = hi(xt_hi[:, at:at + WB * P], xt_ps[:])
                if k % 2 == 0 and k > 0:
                    last = hi(xt_hi[:, 2 * WB * P:], xt_ps[:, 0:P])
                last.then_inc(xt_hi_done, 1)

            def split_w(u):
                act.wait_ge(w_turned, u + 1)
                dst, src = weight_views(u, wgu_hi, wd_hi)
                hi(dst, src).then_inc(w_hi_done, 1)

            def split_h(grp, half, chunks=range(KC), first=False):
                blk = 2 * grp + half
                for i in chunks:
                    act.wait_ge(staged[half][i], LD * OB * (grp + 1))
                    if not first and i < KC - 1:
                        act.wait_ge(h_read, (KC - 1) * (blk - 1) + i + 1)
                    elif not first:
                        act.wait_ge(up_done, FC * blk)
                    hi(h_hi[:, i, :], stage[:, half, i, :]).then_inc(h_hi_done, 1)

            def sigmoid(s, f, first=False):
                act.wait_ge(gate_done, s + 1)
                if not first:
                    act.wait_ge(g_lo_done, s)
                w = width(f)
                act.activation(act_f[0:w, :], gate_ps[0:w, :], ACT.Sigmoid).then_inc(sig_done, 1)

            def split_g(s, f, slot, unused=False):
                act.wait_ge(g_done, s + 1)
                if not unused:
                    act.wait_ge(g_read, s - 1)
                w = width(f)
                hi(g_hi[0:w, slot, :], act_f[0:w, :]).then_inc(g_hi_done, 1)

            def weights(u):
                if u + PERM_AHEAD < E:
                    permute_w(act, hi, u + PERM_AHEAD)
                split_w(u)

            act.wait_ge(consts, 6)
            act.activation(head[0:1, 0:1], ident[0:1, 0:1], ACT.Sigmoid)
            act.wait_ge(setup_t, 1)
            hi(cond_t, gate_ps[:, 0:P]).then_inc(cond_ready, 1)
            act.wait_ge(x_first_loaded[0], LD)
            copy_block(hi, 0, 0)
            split_x(0, 0)
            for v in range(PERM_AHEAD):
                permute_w(act, hi, v)
            split_toep(0)
            for k in range(STEPS):
                if k < STEPS - 1:
                    split_x(0, k + 1)
                for u in early_at(k):
                    weights(u)
                split_h(0, 0, early_h(k), first=True)
            for u in early_at(STEPS):
                weights(u)
            split_h(0, 0, [KC - 2], first=True)
            split_h(0, 0, [KC - 1], first=True)
            sigmoid(0, 0, first=True)
            split_w(number[DOWN, 0])
            split_w(number[DOWN, 1])
            split_g(0, 0, 0, unused=True)

            def ffn_block(g, half, conv, new_w=False):
                for f in range(FC):
                    s, nf = (2 * g + half) * FC + f + 1, (f + 1) % FC
                    if conv or half == 0 or f < FC - 1:
                        sigmoid(s, nf)
                        if new_w:
                            for unit in late_before_up(f):
                                split_w(number[unit])
                        if conv and half == 1 and f == 0:
                            split_toep(g + 1)
                        if conv and half == 1 and f < STEPS:
                            split_x(g + 1, f)
                        if nf == FC - 1 and half == 0:
                            split_h(g, 1)
                        if nf == FC - 1 and half == 1 and conv:
                            split_h(g + 1, 0)
                        split_g(s, nf, (half * FC + f + 1) % 2, unused=new_w and f == 0)
                        if new_w:
                            for unit in late_after_up(f):
                                split_w(number[unit])
                            if EC <= f + 3 < FC:
                                permute_w(act, hi, 2 * (f + 3))

            ffn_block(0, 0, True, new_w=True)
            with act.Fori(0, G - 1) as g:
                ffn_block(g, 1, True)
                ffn_block(g + 1, 0, True)
            ffn_block(G - 1, 1, False)

        @block.vector
        def _(dve):
            def lo(dst, src, hi_part):
                return dve.tensor_tensor(dst, src, hi_part.bitcast(F32), ALU.subtract)

            def copy_ctx_w():
                dve.wait_ge(setup_t, 1)
                dve.tensor_copy(ctx_w_rep, xt_ps[:, P:P + CH].rearrange("d (g a o) -> d g a o", g=G, a=1)
                                .broadcast_to([P, G, R, CG])).then_inc(ctx_w_ready, 1)

            def split_conv_w():
                for n in range(3):
                    rest = xt_ps[0:CG * TAPS, 0:CH] if n == 0 else conv_w_rest[:, n - 1, :]
                    last = dve.tensor_copy(conv_w_t[:, n, :], rest)
                    if n < 2:
                        last.then_inc(parts, 1)
                        dve.wait_ge(parts, 2 * n + 1)
                        dve.tensor_tensor(conv_w_rest[:, n, :], rest, conv_w_t[:, n, :], ALU.subtract).then_inc(parts, 1)
                        dve.wait_ge(parts, 2 * n + 2)
                last.then_inc(conv_w_ready, 1)

            def read_ctx():
                dve.wait_ge(ctx_mm, 1)
                dve.wait_ge(bias_loaded, LD * G)
                dve.tensor_tensor(ctxb[:], conv_ps[:].rearrange("p (g n) -> p g n", g=G),
                                  bias_col[:].broadcast_to([P, G, P]), ALU.add).then_inc(ctx_done, 1)

            def read_toep():
                dve.wait_ge(toep_mm, 1)
                for n, bank in enumerate((gate_ps, up_ps)):
                    q0 = n * (QN // 2)
                    last = dve.tensor_copy(toep[:, :, q0:q0 + QN // 2, :],
                                           bank[:, 0:QN // 2 * CH].rearrange("p (q g o) -> p g q o", g=G, o=CG))
                last.then_inc(toep_done, 1)

            def split_toep(grp):
                if isinstance(grp, int):
                    dve.wait_ge(toep_done, 1)
                dve.wait_ge(t_hi_done, grp + 1)
                lo(ta_lo[:].rearrange("p (q o) -> p q o", o=CG), toep[:, bass.ds(grp, 1), HALO:QN, :],
                   ta_hi[:].rearrange("p (q o) -> p q o", o=CG))
                lo(tb_lo[:, TB0:P], toep[:, bass.ds(grp, 1), 0:HALO, :], tb_hi[:, TB0:P]).then_inc(t_lo_done, 1)

            def split_x(grp, k):
                dve.wait_ge(xt_hi_done, STEPS * grp + k + 1)
                at = (k % 2) * WB * P
                last = lo(xt_lo[:, at:at + WB * P], xt_ps[:], xt_hi[:, at:at + WB * P])
                if k % 2 == 0 and k > 0:
                    last = lo(xt_lo[:, 2 * WB * P:], xt_ps[:, 0:P], xt_hi[:, 2 * WB * P:])
                last.then_inc(xt_lo_done, 1)

            def split_w(u):
                dve.wait_ge(w_hi_done, u + 1)
                dst, src = weight_views(u, wgu_lo, wd_lo)
                hi_part, _ = weight_views(u, wgu_hi, wd_hi)
                lo(dst, src, hi_part).then_inc(w_lo_done, 1)

            def read_head(grp):
                if isinstance(grp, int):
                    dve.wait_ge(ctx_done, 1)
                dve.wait_ge(conv_done, CPG * grp + 1)
                dve.tensor_tensor(head[HEAD0:P, :], conv_ps[HEAD0:P, 0:P], ctxb[HEAD0:P, bass.ds(grp, 1), :],
                                  ALU.add).then_inc(conv_out, 1)

            def read_conv(grp, k):
                i = k // 2
                for half in range(2):
                    if k % 2 == 0 and i > 0 and not isinstance(grp, int):
                        dve.wait_ge(staged[half][i - 1], LD * OB * (grp + 1))
                    elif k % 2 == 0 and not isinstance(grp, int):
                        dve.wait_ge(staged[half][KC - 1], LD * OB * grp)
                if k == 0 and isinstance(grp, int):
                    dve.wait_ge(x_blocked, 2)
                dve.wait_ge(conv_done, CPG * grp + k + 2)
                to = windows(grp, i)
                w0, n = (k % 2) * WB, WB if k < STEPS - 1 else WB - 1
                last = dve.tensor_tensor(to[:, w0:w0 + n, :], conv_bank(grp, k)[:, 0:n * P].rearrange("p (w n) -> p w n", w=n),
                                         ctxb[:, bass.ds(grp, 1), :].broadcast_to([P, n, P]), ALU.add)
                if k == STEPS - 1:
                    dve.tensor_tensor(to[0:HEAD0, JJ - 1, :], conv_bank(grp, k)[0:HEAD0, n * P:(n + 1) * P],
                                      ctxb[0:HEAD0, bass.ds(grp, 1), :], ALU.add)
                    dve.wait_ge(conv_out, CPG * grp + 1)
                    last = dve.tensor_copy(to[HEAD0:P, JJ - 1, :], head[HEAD0:P, :])
                last.then_inc(conv_out, 1)

            def split_h(blk, half, chunks=range(KC)):
                for i in chunks:
                    dve.wait_ge(h_hi_done, KC * blk + i + 1)
                    lo(h_lo[:, i, :], stage[:, half, i, :], h_hi[:, i, :]).then_inc(h_lo_done, 1)

            def silu(s, f):
                dve.wait_ge(sig_done, s + 1)
                w = width(f)
                dve.tensor_tensor(act_f[0:w, :], gate_ps[0:w, :], act_f[0:w, :], ALU.mult).then_inc(silu_done, 1)

            def gated(s, f):
                dve.wait_ge(up_done, s + 1)
                dve.wait_ge(silu_done, s + 1)
                w = width(f)
                dve.tensor_tensor(act_f[0:w, :], up_ps[0:w, :], act_f[0:w, :], ALU.mult).then_inc(g_done, 1)

            def split_g(s, f, slot):
                dve.wait_ge(g_hi_done, s + 1)
                w = width(f)
                lo(g_lo[0:w, slot, :], act_f[0:w, :], g_hi[0:w, slot, :]).then_inc(g_lo_done, 1)

            def add_residual(blk):
                for tt in range(OB):
                    dve.wait_ge(res_loaded[tt], LD * (blk + 1))
                    if tt < OB - 1:
                        dve.wait_ge(y_done, (OB - 1) * blk + tt + 1)
                    else:
                        dve.wait_ge(g_read, FC * (blk + 1))
                    dve.tensor_tensor(res[:, tt, :], acc[:, tt, :], res[:, tt, :], ALU.add).then_inc(acc_free, 1)

            copy_ctx_w()
            split_conv_w()
            read_ctx()
            split_x(0, 0)
            read_toep()
            split_toep(0)
            for k in range(STEPS):
                if k < STEPS - 1:
                    split_x(0, k + 1)
                if k == 0:
                    read_head(0)
                for u in early_at(k):
                    split_w(u)
                read_conv(0, k)
                split_h(0, 0, early_h(k))
            for u in early_at(STEPS):
                split_w(u)
            split_h(0, 0, [KC - 2])
            split_h(0, 0, [KC - 1])
            silu(0, 0)
            split_w(number[DOWN, 0])
            split_w(number[DOWN, 1])
            gated(0, 0)
            split_g(0, 0, 0)

            def ffn_block(g, half, conv, new_w=False):
                blk = 2 * g + half
                for f in range(FC):
                    s, nf = blk * FC + f + 1, (f + 1) % FC
                    if conv or half == 0 or f < FC - 1:
                        silu(s, nf)
                        if new_w:
                            for unit in late_before_up(f):
                                split_w(number[unit])
                        if conv and half == 1 and f == 0:
                            split_toep(g + 1)
                        if conv and half == 1 and f < STEPS:
                            split_x(g + 1, f)
                        if nf == FC - 1 and (half == 0 or conv):
                            split_h(blk + 1, 1 - half)
                        gated(s, nf)
                        if conv and half == 1 and f == 0:
                            read_head(g + 1)
                        if conv and half == 1 and 1 <= f <= STEPS:
                            read_conv(g + 1, f - 1)
                        split_g(s, nf, (half * FC + f + 1) % 2)
                        if new_w:
                            for unit in late_after_up(f):
                                split_w(number[unit])
                add_residual(blk)

            ffn_block(0, 0, True, new_w=True)
            with dve.Fori(0, G - 1) as g:
                ffn_block(g, 1, True)
                ffn_block(g + 1, 0, True)
            ffn_block(G - 1, 1, False)


_INS = ["x", "cond_128", "fside_S_0", "L0_cond_weight", "L0_cond_c_weight", "L0_ffn_W_gate", "L0_ffn_W_up", "L0_ffn_W_down"]


def kernel(**inputs):
    import numpy as np
    import concourse.bacc as bacc
    from concourse.bass_utils import run_bass_kernel_spmd

    nc = bacc.Bacc("TRN2", target_bir_lowering=False, num_devices=1)
    arrays, args = {}, []
    for name in _INS:
        a = np.ascontiguousarray(inputs[name])
        arrays[f"in_{name}"] = a
        args.append(nc.dram_tensor(f"in_{name}", a.shape, mybir.dt.from_np(a.dtype), kind="ExternalInput").ap())
    args.append(nc.dram_tensor("out_y", inputs["x"].shape, F32, kind="ExternalOutput").ap())
    adaln_ffn(nc, *args)
    r = run_bass_kernel_spmd(nc, [arrays], core_ids=[0])
    return r.results[0]["out_y"]
```
